# Optimizing a Trainium2 kernel written in Bass

```python
import numpy as np
import jax
import jax.numpy as jnp

def _softmax(x, axis=-1):
    return jax.nn.softmax(x, axis=axis)

def _gelu(x):
    return jax.nn.gelu(x, approximate=True)

def _silu(x):
    return jax.nn.silu(x)

def _sigmoid(x):
    return jax.nn.sigmoid(x)

def _layernorm(x, axis=-1, eps=1e-05):
    m = jnp.mean(x, axis=axis, keepdims=True)
    v = jnp.var(x, axis=axis, keepdims=True)
    return (x - m) / jnp.sqrt(v + eps)

def _scatter_add(tgt, idx, src, axis=0):
    return tgt.at[idx].add(src)

def _segment_sum(src, seg, n):
    return jax.ops.segment_sum(src, seg, n)
kernel_name = 'mk_seq_preln_d1_jaxref_r4_ec02d0'

def setup_inputs(seed: int=0):
    np.random.seed(seed)
    _w = jnp.asarray

    def _L0_attn_setup():
        import jax, jax.numpy as jnp
        import numpy as np
        B, C, D_MODEL, N_HEADS = (2, 512, 256, 16)

        def rotary_matrix(context_length: int, d: int) -> jnp.ndarray:
            half = d // 2
            i = jnp.arange(half, dtype=jnp.float32)
            theta = 10000.0 ** (-2.0 * (i - 1.0) / d)
            m = jnp.arange(context_length, dtype=jnp.float32)
            ang = m[:, None] * theta
            c, s = (jnp.cos(ang), jnp.sin(ang))
            ev = 2 * jnp.arange(half)
            od = ev + 1
            R = jnp.zeros((context_length, d, d), jnp.float32)
            R = R.at[:, ev, ev].set(c)
            R = R.at[:, ev, od].set(-s)
            R = R.at[:, od, ev].set(s)
            R = R.at[:, od, od].set(c)
            return R
        key = jax.random.key(seed)
        k1, k2, k3, k4 = jax.random.split(key, 4)
        x = jax.random.normal(k1, (B, C, D_MODEL), dtype=jnp.float32)
        w_qkv = jax.random.normal(k2, (3 * D_MODEL, D_MODEL), dtype=jnp.float32) * 0.02
        w_out = jax.random.normal(k3, (D_MODEL, D_MODEL), dtype=jnp.float32) * 0.02
        b_out = jax.random.normal(k4, (D_MODEL,), dtype=jnp.float32) * 0.02
        return {'x': x, 'w_qkv': w_qkv, 'w_out': w_out, 'b_out': b_out}
    _L0_attn_in = _L0_attn_setup()

    def _L0_ffn_setup():
        import jax, jax.numpy as jnp
        import numpy as np
        D_MODEL = 256
        N_HEADS = 16
        HEAD_DIM = D_MODEL // N_HEADS
        KV_LATENT = 128
        N_EXPERTS = 4
        D_HIDDEN = 4 * D_MODEL
        B, T = (2, 256)

        def rmsnorm(x, w, eps=1e-06):
            return w * (x * jax.lax.rsqrt(jnp.mean(x * x, axis=-1, keepdims=True) + eps))

        def layernorm(x, g, b, eps=1e-05):
            mu = jnp.mean(x, axis=-1, keepdims=True)
            var = jnp.mean((x - mu) ** 2, axis=-1, keepdims=True)
            return (x - mu) * jax.lax.rsqrt(var + eps) * g + b

        def apply_rope(x):
            t, d = (x.shape[2], x.shape[3])
            half = d // 2
            pos = jnp.arange(t, dtype=x.dtype)[:, None]
            inv_freq = 1.0 / 10000.0 ** (jnp.arange(half, dtype=x.dtype) / half)
            ang = pos * inv_freq[None, :]
            sin, cos = (jnp.sin(ang), jnp.cos(ang))
            x1, x2 = (x[..., :half], x[..., half:])
            return jnp.concatenate([x1 * cos - x2 * sin, x1 * sin + x2 * cos], axis=-1)

        def mla_attention(x, Wq, Wdkv, Wuk, Wuv, Wo, ln_g, ln_b):
            b, t, _ = x.shape
            q = (x @ Wq.T).reshape(b, t, N_HEADS, HEAD_DIM).transpose(0, 2, 1, 3)
            latent = layernorm(x @ Wdkv.T, ln_g, ln_b)
            k = (latent @ Wuk.T).reshape(b, t, N_HEADS, HEAD_DIM).transpose(0, 2, 1, 3)
            v = (latent @ Wuv.T).reshape(b, t, N_HEADS, HEAD_DIM).transpose(0, 2, 1, 3)
            q = apply_rope(q)
            k = apply_rope(k)
            scores = jnp.einsum('bhqd,bhkd->bhqk', q, k) / np.sqrt(HEAD_DIM)
            causal = jnp.tril(jnp.ones((t, t), dtype=bool))
            scores = jnp.where(causal, scores, -jnp.inf)
            attn = jax.nn.softmax(scores, axis=-1)
            out = jnp.einsum('bhqk,bhkd->bhqd', attn, v).transpose(0, 2, 1, 3).reshape(b, t, D_MODEL)
            return out @ Wo.T

        def moe(x, gate_w, gate_b, W1, b1, W2, b2):
            logits = x @ gate_w.T + gate_b
            top = jnp.argmax(logits, axis=-1)
            onehot = jax.nn.one_hot(top, N_EXPERTS, dtype=x.dtype)
            h = jax.nn.relu(jnp.einsum('btd,ehd->bteh', x, W1) + b1)
            y = jnp.einsum('bteh,edh->bted', h, W2) + b2
            return jnp.einsum('bted,bte->btd', y, onehot)
        key = jax.random.key(seed)
        ks = jax.random.split(key, 16)
        s = lambda fan_in: 1.0 / np.sqrt(fan_in)
        return {'x': jax.random.normal(ks[0], (B, T, D_MODEL), jnp.float32), 'norm1_w': jnp.ones((D_MODEL,), jnp.float32), 'norm2_w': jnp.ones((D_MODEL,), jnp.float32), 'Wq': jax.random.normal(ks[1], (D_MODEL, D_MODEL), jnp.float32) * s(D_MODEL), 'Wdkv': jax.random.normal(ks[2], (KV_LATENT, D_MODEL), jnp.float32) * s(D_MODEL), 'Wuk': jax.random.normal(ks[3], (D_MODEL, KV_LATENT), jnp.float32) * s(KV_LATENT), 'Wuv': jax.random.normal(ks[4], (D_MODEL, KV_LATENT), jnp.float32) * s(KV_LATENT), 'Wo': jax.random.normal(ks[5], (D_MODEL, D_MODEL), jnp.float32) * s(D_MODEL), 'ln_g': jnp.ones((KV_LATENT,), jnp.float32), 'ln_b': jnp.zeros((KV_LATENT,), jnp.float32), 'gate_w': jax.random.normal(ks[6], (N_EXPERTS, D_MODEL), jnp.float32) * s(D_MODEL), 'gate_b': jnp.zeros((N_EXPERTS,), jnp.float32), 'W1': jax.random.normal(ks[7], (N_EXPERTS, D_HIDDEN, D_MODEL), jnp.float32) * s(D_MODEL), 'b1': jnp.zeros((N_EXPERTS, D_HIDDEN), jnp.float32), 'W2': jax.random.normal(ks[8], (N_EXPERTS, D_MODEL, D_HIDDEN), jnp.float32) * s(D_HIDDEN), 'b2': jnp.zeros((N_EXPERTS, D_MODEL), jnp.float32)}
    _L0_ffn_in = _L0_ffn_setup()
    _d = {'L0_attn_x': _L0_attn_in['x'], 'L0_attn_w_qkv': _L0_attn_in['w_qkv'], 'L0_attn_w_out': _L0_attn_in['w_out'], 'L0_attn_b_out': _L0_attn_in['b_out'], 'L0_ffn_norm1_w': _L0_ffn_in['norm1_w'], 'L0_ffn_norm2_w': _L0_ffn_in['norm2_w'], 'L0_ffn_Wq': _L0_ffn_in['Wq'], 'L0_ffn_Wdkv': _L0_ffn_in['Wdkv'], 'L0_ffn_Wuk': _L0_ffn_in['Wuk'], 'L0_ffn_Wuv': _L0_ffn_in['Wuv'], 'L0_ffn_Wo': _L0_ffn_in['Wo'], 'L0_ffn_ln_g': _L0_ffn_in['ln_g'], 'L0_ffn_ln_b': _L0_ffn_in['ln_b'], 'L0_ffn_gate_w': _L0_ffn_in['gate_w'], 'L0_ffn_gate_b': _L0_ffn_in['gate_b'], 'L0_ffn_W1': _L0_ffn_in['W1'], 'L0_ffn_b1': _L0_ffn_in['b1'], 'L0_ffn_W2': _L0_ffn_in['W2'], 'L0_ffn_b2': _L0_ffn_in['b2']}
    _x0 = _d['L0_attn_x']
    _d['L0_attn_x'] = jax.random.normal(jax.random.fold_in(jax.random.key(seed), 1), (8, 1024, 256), dtype=_x0.dtype)
    del _x0
    return _d

def reference(L0_attn_x, L0_attn_w_qkv, L0_attn_w_out, L0_attn_b_out, L0_ffn_norm1_w, L0_ffn_norm2_w, L0_ffn_Wq, L0_ffn_Wdkv, L0_ffn_Wuk, L0_ffn_Wuv, L0_ffn_Wo, L0_ffn_ln_g, L0_ffn_ln_b, L0_ffn_gate_w, L0_ffn_gate_b, L0_ffn_W1, L0_ffn_b1, L0_ffn_W2, L0_ffn_b2):

    def _L0_attn_ref(x, w_qkv, w_out, b_out):
        import jax, jax.numpy as jnp
        import numpy as np
        B, C, D_MODEL, N_HEADS = (2, 512, 256, 16)

        def rotary_matrix(context_length: int, d: int) -> jnp.ndarray:
            half = d // 2
            i = jnp.arange(half, dtype=jnp.float32)
            theta = 10000.0 ** (-2.0 * (i - 1.0) / d)
            m = jnp.arange(context_length, dtype=jnp.float32)
            ang = m[:, None] * theta
            c, s = (jnp.cos(ang), jnp.sin(ang))
            ev = 2 * jnp.arange(half)
            od = ev + 1
            R = jnp.zeros((context_length, d, d), jnp.float32)
            R = R.at[:, ev, ev].set(c)
            R = R.at[:, ev, od].set(-s)
            R = R.at[:, od, ev].set(s)
            R = R.at[:, od, od].set(c)
            return R
        b, c, d = x.shape
        h = N_HEADS
        dh = d // h
        qkv = x @ w_qkv.T
        q, k, v = jnp.split(qkv, 3, axis=-1)
        q = q.reshape(b, c, h, dh).transpose(0, 2, 1, 3)
        k = k.reshape(b, c, h, dh).transpose(0, 2, 1, 3)
        v = v.reshape(b, c, h, dh).transpose(0, 2, 1, 3)
        R = rotary_matrix(c, dh)
        q_rot = jnp.einsum('bhci,cij->bhcj', q, R)
        k_rot = jnp.einsum('bhci,cij->bhcj', k, R)
        scale = jnp.sqrt(jnp.float32(dh))
        attn_num = jnp.exp(jnp.einsum('bhqd,bhkd->bhqk', q_rot, k_rot) / scale)
        attn_den = jnp.exp(jnp.einsum('bhqd,bhkd->bhqk', q, k) / scale)
        attn_den = jnp.sum(attn_den, axis=-1, keepdims=True)
        attn = attn_num / attn_den
        causal = jnp.tril(jnp.ones((c, c), jnp.float32))[None, None]
        attn = jnp.where(causal == 0, 0.0, attn)
        y = jnp.einsum('bhqk,bhkd->bhqd', attn, v)
        y = y.transpose(0, 2, 1, 3).reshape(b, c, d)
        return y @ w_out.T + b_out

    def _L0_ffn_ref(x, norm1_w, norm2_w, Wq, Wdkv, Wuk, Wuv, Wo, ln_g, ln_b, gate_w, gate_b, W1, b1, W2, b2):
        import jax, jax.numpy as jnp
        import numpy as np
        D_MODEL = 256
        N_HEADS = 16
        HEAD_DIM = D_MODEL // N_HEADS
        KV_LATENT = 128
        N_EXPERTS = 4
        D_HIDDEN = 4 * D_MODEL
        B, T = (2, 256)

        def rmsnorm(x, w, eps=1e-06):
            return w * (x * jax.lax.rsqrt(jnp.mean(x * x, axis=-1, keepdims=True) + eps))

        def layernorm(x, g, b, eps=1e-05):
            mu = jnp.mean(x, axis=-1, keepdims=True)
            var = jnp.mean((x - mu) ** 2, axis=-1, keepdims=True)
            return (x - mu) * jax.lax.rsqrt(var + eps) * g + b

        def apply_rope(x):
            t, d = (x.shape[2], x.shape[3])
            half = d // 2
            pos = jnp.arange(t, dtype=x.dtype)[:, None]
            inv_freq = 1.0 / 10000.0 ** (jnp.arange(half, dtype=x.dtype) / half)
            ang = pos * inv_freq[None, :]
            sin, cos = (jnp.sin(ang), jnp.cos(ang))
            x1, x2 = (x[..., :half], x[..., half:])
            return jnp.concatenate([x1 * cos - x2 * sin, x1 * sin + x2 * cos], axis=-1)

        def mla_attention(x, Wq, Wdkv, Wuk, Wuv, Wo, ln_g, ln_b):
            b, t, _ = x.shape
            q = (x @ Wq.T).reshape(b, t, N_HEADS, HEAD_DIM).transpose(0, 2, 1, 3)
            latent = layernorm(x @ Wdkv.T, ln_g, ln_b)
            k = (latent @ Wuk.T).reshape(b, t, N_HEADS, HEAD_DIM).transpose(0, 2, 1, 3)
            v = (latent @ Wuv.T).reshape(b, t, N_HEADS, HEAD_DIM).transpose(0, 2, 1, 3)
            q = apply_rope(q)
            k = apply_rope(k)
            scores = jnp.einsum('bhqd,bhkd->bhqk', q, k) / np.sqrt(HEAD_DIM)
            causal = jnp.tril(jnp.ones((t, t), dtype=bool))
            scores = jnp.where(causal, scores, -jnp.inf)
            attn = jax.nn.softmax(scores, axis=-1)
            out = jnp.einsum('bhqk,bhkd->bhqd', attn, v).transpose(0, 2, 1, 3).reshape(b, t, D_MODEL)
            return out @ Wo.T

        def moe(x, gate_w, gate_b, W1, b1, W2, b2):
            logits = x @ gate_w.T + gate_b
            top = jnp.argmax(logits, axis=-1)
            onehot = jax.nn.one_hot(top, N_EXPERTS, dtype=x.dtype)
            h = jax.nn.relu(jnp.einsum('btd,ehd->bteh', x, W1) + b1)
            y = jnp.einsum('bteh,edh->bted', h, W2) + b2
            return jnp.einsum('bted,bte->btd', y, onehot)
        x = x + mla_attention(rmsnorm(x, norm1_w), Wq, Wdkv, Wuk, Wuv, Wo, ln_g, ln_b)
        x = x + moe(rmsnorm(x, norm2_w), gate_w, gate_b, W1, b1, W2, b2)
        return x
    x = L0_attn_x
    x = x + _L0_attn_ref(_layernorm(x, axis=-1), L0_attn_w_qkv, L0_attn_w_out, L0_attn_b_out)
    x = x + _L0_ffn_ref(_layernorm(x, axis=-1), L0_ffn_norm1_w, L0_ffn_norm2_w, L0_ffn_Wq, L0_ffn_Wdkv, L0_ffn_Wuk, L0_ffn_Wuv, L0_ffn_Wo, L0_ffn_ln_g, L0_ffn_ln_b, L0_ffn_gate_w, L0_ffn_gate_b, L0_ffn_W1, L0_ffn_b1, L0_ffn_W2, L0_ffn_b2)
    return x

_drawn_inputs = setup_inputs


def setup_inputs(seed=0):
    import zlib

    import numpy as np

    out = dict(_drawn_inputs(seed))
    spreads = {'L0_ffn_norm1_w': (1.0, 0.2),
     'L0_ffn_norm2_w': (1.0, 0.2),
     'L0_ffn_ln_g': (1.0, 0.2),
     'L0_ffn_ln_b': (0.0, 0.1),
     'L0_ffn_gate_b': (0.0, 0.1),
     'L0_ffn_b1': (0.0, 0.1),
     'L0_ffn_b2': (0.0, 0.1)}
    factors = {}
    for name, (base, spread) in spreads.items():
        noise = np.random.default_rng([zlib.crc32(name.encode()), seed]).standard_normal(out[name].shape)
        drawn = base * np.exp(spread * noise) if base else spread * noise
        out[name] = jnp.asarray(drawn.astype(out[name].dtype))
    for name, factor in factors.items():
        out[name] = (out[name] * factor).astype(out[name].dtype)
    return out
```

```python
from contextlib import ExitStack

import concourse.bass as bass
from concourse import mybir

P = 128
D = 256
HEADS, HD = 16, 16
LAT = 128
EXPERTS, HID = 4, 1024
B, T = 8, 1024
TT = T // P
DC = D // P
HC = HID // P
HALF = 512
GROUP = 4
GROUPS = HEADS // GROUP
VC = P // GROUP
PARTS = 3
TERMS = [(0, 0), (1, 0), (2, 0), (0, 1), (1, 1), (0, 2)]
STACK = len(TERMS) * HD
SCALE = 1.0 / 4.0
MASKED = -1e30
SLOTS = 3

F32 = mybir.dt.float32
BF16 = mybir.dt.bfloat16
ALU = mybir.AluOpType
ACT = mybir.ActivationFunctionType
AX_X = mybir.AxisListType.X

STEPS = []
for _h in range(2):
    for _kb in range(4 * _h + 4):
        _lo = max(_kb * P, _h * HALF)
        STEPS.append((_h, _kb, _lo, (_h + 1) * HALF - _lo))
NSTEP = len(STEPS)
NALL = GROUPS * NSTEP


def attention_schedule(a):
    items = []
    if a == 1:
        items += [("max", a, 0, j, qb) for j in range(GROUP) for qb in range(TT)]
        items.append(("mx", a, 0))
    for s in range(NALL):
        g, i = divmod(s, NSTEP)
        half = STEPS[i][0]
        items += [("num", a, s, pair) for pair in range(2)]
        if a == 0:
            per = 16 // (4 * half + 4)
            at = per * (i - 4 * half)
            items += [("den", a, g, n % GROUP, 4 * half + n // GROUP) for n in range(at, at + per)]
        if s >= 1:
            items.append(("pv", a, s - 1))
        if s >= 2 and closes(s - 2):
            items.append(("ot", a, (s - 2) // NSTEP, STEPS[(s - 2) % NSTEP][0]))
        if a == 1 and g + 1 < GROUPS and 2 <= i < 10:
            items += [("max", a, g + 1, n // TT, n % TT) for n in range(4 * (i - 2), 4 * (i - 1))]
        elif a == 1 and g + 1 < GROUPS and i == 10:
            items.append(("mx", a, g + 1))
    items.append(("pv", a, NALL - 1))
    items.append(("ot", a, GROUPS - 1, 1))
    return items


def closes(s):
    i = s % NSTEP
    return i == NSTEP - 1 or STEPS[i + 1][0] != STEPS[i][0]


UNITS = [("q", 0), ("k", 0), ("q", 1), ("k", 1)]
NU = len(UNITS)

SCHED = [attention_schedule(0), attention_schedule(1)]


def plan_slots():
    uses = [("xt", 0, c) for c in range(DC)]
    uses += [("proj", 0, 0), ("proj", 0, 1)]
    for u in range(NU):
        uses.append(("swap", 0, u))
        if u + 2 < NU:
            uses.append(("proj", 0, u + 2))
    uses += [("v", 0, h) for h in range(2)]
    uses += [x for x in SCHED[0] if x[0] in ("num", "den")]
    uses += [("yt", 0, c) for c in range(DC)] + [("op", 0, h) for h in range(2)]
    uses += [("xt", 1, c) for c in range(DC)]
    uses += [("lat",), ("proj", 1, 0), ("proj", 1, 2), ("lt",), ("swap", 1, 0), ("swap", 1, 2)]
    uses += [("proj", 1, 1), ("proj", 1, 3), ("swap", 1, 1), ("swap", 1, 3)]
    uses += [("v", 1, h) for h in range(2)]
    uses += [x for x in SCHED[1] if x[0] in ("num", "max")]
    uses += [("yt", 1, c) for c in range(DC)] + [("op", 1, h) for h in range(2)]
    uses += [("xt", 2, c) for c in range(DC)]
    uses += [("gate",), ("oht",)] + [("b2", h) for h in range(2)]
    for e in range(EXPERTS):
        uses += [("h", e, h, n) for h in range(2) for n in range(HC // 2)]
        uses += [("y", e, h) for h in range(2)]
    return {key: n for n, key in enumerate(uses)}


ORDER = [[0, 1, 2, 3], [0, 2, 1, 3]]
SLOT = plan_slots()
BANK = {x: n for n, x in enumerate(x for a in range(2) for x in SCHED[a] if x[0] in ("ot", "mx"))}
HALVES = {x: n for n, x in enumerate(("pv", a, s) for a in range(2) for s in range(NALL) if closes(s))}


def jobs_before(a, n, rotated):
    return 2 * n + rotated if a == 0 else 2 * NU + n


def build(nc, x, wqkv, wout, bout, norms, wq, wdkv, wuk, wuv, wo, lnp, gate, gate_b, w1, b1, w2, b2,
          cos, sin, perm, ident_f, ident_b, mask_b, out):
    scratch = nc.dram_tensor("head_parts", (6, HEADS, PARTS, HD, T), BF16, kind="Internal").ap()
    max_scratch = nc.dram_tensor("max_parts", (2, PARTS, GROUP, T), BF16, kind="Internal").ap()

    with ExitStack() as ctx:
        def sb(name, shape, dt=F32):
            return ctx.enter_context(nc.sbuf_tensor(name, shape, dt))

        def sem(name):
            return ctx.enter_context(nc.semaphore(name))

        slots = [ctx.enter_context(nc.psum_tensor(f"slot{i}", [P, 2 * HALF], F32)) for i in range(SLOTS)]
        o_bank = ctx.enter_context(nc.psum_tensor("o_bank", [P, HALF], F32))
        t_bank = ctx.enter_context(nc.psum_tensor("t_bank", [P, HALF], F32))

        wqkv_sb = sb("wqkv_sb", [P, DC, 3 * D])
        wout_sb = sb("wout_sb", [P, DC, D])
        wq_sb = sb("wq_sb", [P, DC, D])
        wdkv_sb = sb("wdkv_sb", [P, DC, LAT])
        wuk_sb = sb("wuk_sb", [P, D])
        wuv_sb = sb("wuv_sb", [P, D])
        wo_sb = sb("wo_sb", [P, DC, D])
        gate_sb = sb("gate_sb", [P, DC, EXPERTS])
        bout_sb = sb("bout_sb", [P, D])
        gate_b_sb = sb("gate_b_sb", [P, EXPERTS])
        norms_sb = sb("norms_sb", [P, 2, DC])
        ln_sb = sb("ln_sb", [P, 2])
        b1_sb = sb("b1_sb", [P, EXPERTS, HC])
        b2_sb = sb("b2_sb", [EXPERTS, D])
        cos_sb = sb("cos_sb", [P, 2, T])
        sin_sb = sb("sin_sb", [P, 2, T])
        perm_sb = sb("perm_sb", [P, 2, P])
        idf = sb("idf", [P, P])
        idb = sb("idb", [P, P], BF16)
        mask_sb = sb("mask_sb", [P, 2, P], BF16)

        xs = sb("xs", [P, TT, D])
        xn = sb("xn", [P, TT, D])
        zs = sb("zs", [P, TT, D])
        xt = sb("xt", [P, DC, T])
        tmp = sb("tmp", [P, 4 * T])
        qs = [tmp[:, 0:T], tmp[:, T:2 * T]]
        cosq = tmp[:, 2 * T:3 * T]
        rot = tmp[:, 3 * T:4 * T]
        rest = sb("rest", [P, T])
        parts = sb("parts", [P, 2, PARTS, T], BF16)
        vs = sb("vs", [P, TT, HEADS, VC])
        plain = sb("plain", [P, 2, 2, GROUP * T], BF16)
        turned = sb("turned", [P, 2, 2, GROUP * T], BF16)
        prob = sb("prob", [P, 2, GROUP * HALF])
        o_sb = sb("o_sb", [P, 2, HALF])
        sums = sb("sums", [P, TT, HEADS])
        recip = sb("recip", [P, 16])
        stats = sb("stats", [P, TT, 6])
        mv = sb("mv", [P, TT, 2])
        t8 = sb("t8", [P, 6, TT])
        latn, latt = xn[:, :, :].rearrange("p t d -> p (t d)")[:, 0:T], xn[:, :, :].rearrange("p t d -> p (t d)")[:, T:2 * T]
        maxes = sb("maxes", [P, GROUP * TT])
        mrow = sb("mrow", [GROUP * TT, 2, P])
        mpart = sb("mpart", [GROUP * TT, PARTS, P], BF16)
        logits = sb("logits", [P, TT, EXPERTS])
        top = sb("top", [P, TT])
        onehot = sb("onehot", [P, TT, EXPERTS])
        oht = sb("oht", [EXPERTS, T])
        hidden = [prob[:, :, :].rearrange("p a n -> p (a n)"), tmp[:, :]]
        expert = [plain[:, i].rearrange("p a n -> p (a n)").bitcast(F32) for i in range(2)]

        s_const = sem("s_const")
        values_padded = sem("values_padded")
        ones_written = sem("ones_written")
        slot_filled = [sem(f"slot_filled{i}") for i in range(SLOTS)]
        slot_drained = [sem(f"slot_drained{i}") for i in range(SLOTS)]
        x_landed = sem("x_landed")
        v_step = sem("v_step")
        var_ready = sem("var_ready")
        std_ready = sem("std_ready")
        normed = sem("normed")
        bias_added = sem("bias_added")
        cos_done = sem("cos_done")
        rot_done = sem("rot_done")
        split_done = sem("split_done")
        onehot_ready = sem("onehot_ready")
        parts_out = [sem(f"parts_out{i}") for i in range(2)]
        stack_in = [sem(f"stack_in{i}") for i in range(2)]
        pv_done = sem("pv_done")
        o_filled = sem("o_filled")
        o_drained = sem("o_drained")
        t_filled = sem("t_filled")
        t_drained = sem("t_drained")
        max_split = sem("max_split")
        max_out = sem("max_out")
        max_in = [sem(f"max_in{i}") for i in range(2)]
        xr_done = sem("xr_done")
        w_landed = [sem(f"w_landed{i}") for i in range(2)]
        out_done = sem("out_done")
        in_loop = ([x_landed, v_step, var_ready, std_ready, normed, bias_added, cos_done,
                    rot_done, split_done, onehot_ready, pv_done, o_filled, o_drained, t_filled, t_drained,
                    max_split, max_out, xr_done, out_done] + slot_filled + slot_drained
                   + parts_out + stack_in + max_in + w_landed)

        def filled(eng, key):
            n = SLOT[key]
            eng.wait_ge(slot_filled[n % SLOTS], n // SLOTS + 1)
            return slots[n % SLOTS]

        def wait_drained(eng, key):
            n = SLOT[key]
            eng.wait_ge(slot_drained[n % SLOTS], n // SLOTS + 1)

        def drained(key):
            return slot_drained[SLOT[key] % SLOTS]

        consts = [(wqkv_sb, wqkv), (wout_sb, wout), (wq_sb, wq), (wdkv_sb, wdkv), (wuk_sb, wuk), (wuv_sb, wuv),
                  (wo_sb, wo), (gate_sb, gate), (bout_sb, bout), (gate_b_sb, gate_b), (norms_sb, norms),
                  (ln_sb, lnp), (b1_sb, b1), (b2_sb, b2), (cos_sb, cos), (sin_sb, sin), (perm_sb, perm),
                  (idf, ident_f), (idb, ident_b), (mask_sb, mask_b)]
        with nc.Block(no_gpsimd_drain=True) as block:
            @block.sync
            def _(sp):
                for dst, src in consts:
                    sp.dma_start(dst[:], src).then_inc(s_const, 16)
                sp.wait_ge(s_const, 16 * len(consts))

            @block.vector
            def _(dve):
                nc.vector.memset(vs[:], 0.0).then_inc(values_padded, 1)
                dve.wait_ge(values_padded, 1)
                nc.vector.memset(vs[:, :, :, HD:HD + 1], 1.0).then_inc(values_padded, 1)
                dve.wait_ge(values_padded, 2)

            @block.gpsimd
            def _(pool):
                for par in range(2):
                    nc.gpsimd.memset(turned[STACK:STACK + PARTS, par, 1, :], 1.0).then_inc(ones_written, 1)
                pool.wait_ge(ones_written, 2)

        with nc.Fori(0, B, 1) as b:
            with nc.Block(no_gpsimd_drain=True) as block:
                x_b = x[bass.ds(b, 1)].rearrange("b (t p) d -> p (b t) d", p=P)
                out_b = out[bass.ds(b, 1)].rearrange("b (t p) d -> p (b t) d", p=P)

                @block.sync
                def _(sp):
                    sp.dma_start(xs[:], x_b).then_inc(x_landed, 16)

                    def store_parts(a, n, rotated):
                        tensor, blk = UNITS[ORDER[a][n]]
                        job = jobs_before(a, n, rotated)
                        row = 4 * a + 2 * rotated * (1 - a) + (tensor == "k")
                        sp.wait_ge(split_done, job + 1)
                        for t in range(PARTS):
                            sp.dma_start(scratch[row, 8 * blk:8 * blk + 8, t],
                                         parts[:, job % 2, t, :]).then_inc(parts_out[job % 2], 16)

                    def load_stack(dst, row, g, side, par):
                        h0 = GROUP * g
                        at = 0
                        for term in ([[0, 1, 2], [0, 1], [0]] if side == 0 else [[0], [0], [0], [1], [1], [2]]):
                            n = len(term) * HD
                            src = scratch[row, h0:h0 + GROUP, term[0]:term[-1] + 1].rearrange("h t d n -> (t d) h n")
                            sp.dma_start(dst[at:at + n, :].rearrange("p (h n) -> p h n", h=GROUP),
                                         src).then_inc(stack_in[par], 16)
                            at += n

                    def load_group(a, g):
                        par = g % 2
                        if a == 0:
                            if g >= 2:
                                sp.wait_ge(pv_done, NSTEP * (g - 1))
                            for par_out in range(2):
                                sp.wait_ge(parts_out[par_out], 16 * PARTS * (2 if g < 2 else 4))
                            for side in range(2):
                                load_stack(plain[:, par, side], side, g, side, par)
                                load_stack(turned[:, par, side], 2 + side, g, side, par)
                        else:
                            sp.wait_ge(pv_done, NSTEP * (GROUPS + g - 1))
                            for par_out in range(2):
                                sp.wait_ge(parts_out[par_out], 16 * PARTS * 6)
                            for side in range(2):
                                load_stack(turned[:, par, side], 4 + side, g, side, par)

                    for n in range(2):
                        store_parts(0, n, 0)
                        store_parts(0, n, 1)
                    load_group(0, 0)
                    load_group(0, 1)
                    for n in range(2, 4):
                        store_parts(0, n, 0)
                        store_parts(0, n, 1)
                    load_group(0, 2)
                    load_group(0, 3)

                    def load_expert(e):
                        sp.dma_start(expert[e % 2][:, 0:DC * HID], w1[e]).then_inc(w_landed[e % 2], 16)
                        sp.dma_start(expert[e % 2][:, DC * HID:], w2[e]).then_inc(w_landed[e % 2], 16)

                    sp.wait_ge(pv_done, NALL)
                    load_expert(0)
                    load_expert(1)
                    for n in range(4):
                        store_parts(1, n, 1)

                    def move_max(g):
                        par = g % 2
                        sp.wait_ge(max_split, g + 1)
                        for t in range(PARTS):
                            sp.dma_start(max_scratch[par, t].rearrange("j (r n) -> (j r) n", n=P),
                                         mpart[:, t, :]).then_inc(max_out, 16)
                        sp.wait_ge(max_out, 16 * PARTS * (g + 1))
                        sp.dma_start(turned[STACK:STACK + PARTS, par, 0, :].rearrange("p (h n) -> p h n", h=GROUP),
                                     max_scratch[par]).then_inc(max_in[par], 16)

                    load_group(1, 0)
                    load_group(1, 1)
                    move_max(0)
                    move_max(1)
                    load_group(1, 2)
                    move_max(2)
                    load_group(1, 3)
                    move_max(3)
                    for e in range(2, EXPERTS):
                        wait_drained(sp, ("y", e - 2, 1))
                        load_expert(e)
                    for h in range(2):
                        wait_drained(sp, ("y", EXPERTS - 1, h))
                    sp.dma_start(out_b, xs[:]).then_inc(out_done, 16)
                    sp.wait_ge(out_done, 16)

                @block.tensor
                def _(pe):
                    def take(key):
                        n = SLOT[key]
                        if n >= SLOTS:
                            pe.wait_ge(slot_drained[n % SLOTS], n // SLOTS)
                        return slots[n % SLOTS]

                    def give(key, ins):
                        ins.then_inc(slot_filled[SLOT[key] % SLOTS], 1)

                    def transposes(key, src):
                        slot = take(key)
                        for t in range(TT):
                            last = nc.tensor.transpose(slot[:, t * P:(t + 1) * P], src(t), idf[:])
                        give(key, last)

                    def project(a, u):
                        tensor, blk = UNITS[u]
                        key = ("proj", a, u)
                        slot = take(key)
                        for half in range(2):
                            cols = slice(half * HALF, (half + 1) * HALF)
                            if a == 1 and tensor == "k":
                                pairs = [(wuk_sb[:, blk * P:(blk + 1) * P], latt[:, cols])]
                            elif a == 1:
                                pairs = [(wq_sb[:, c, blk * P:(blk + 1) * P], xt[:, c, cols]) for c in range(DC)]
                            else:
                                at = (tensor == "k") * D + blk * P
                                pairs = [(wqkv_sb[:, c, at:at + P], xt[:, c, cols]) for c in range(DC)]
                            for c, (w, r) in enumerate(pairs):
                                last = nc.tensor.matmul(slot[:, cols], w, r, start=c == 0, stop=c == len(pairs) - 1)
                        give(key, last)

                    def swap(a, n):
                        u = ORDER[a][n]
                        key = ("swap", a, u)
                        wait_drained(pe, ("proj", a, u))
                        slot = take(key)
                        for half in range(2):
                            cols = slice(half * HALF, (half + 1) * HALF)
                            last = nc.tensor.matmul(slot[:, cols], perm_sb[:, a, :], qs[n % 2][:, cols],
                                                    start=True, stop=True)
                        give(key, last)

                    def values(a):
                        for h in range(2):
                            key = ("v", a, h)
                            slot = take(key)
                            for i in range(4):
                                t = 4 * h + i
                                if a == 0:
                                    pairs = [(xt[:, c, t * P:(t + 1) * P], wqkv_sb[:, c, 2 * D:3 * D])
                                             for c in range(DC)]
                                else:
                                    pairs = [(latt[:, t * P:(t + 1) * P], wuv_sb[:])]
                                for c, (l, r) in enumerate(pairs):
                                    last = nc.tensor.matmul(slot[:, i * D:(i + 1) * D], l, r,
                                                            start=c == 0, stop=c == len(pairs) - 1)
                            give(key, last)

                    def out_project(a, w):
                        for h in range(2):
                            key = ("op", a, h)
                            slot = take(key)
                            for i in range(4):
                                t = 4 * h + i
                                for c in range(DC):
                                    last = nc.tensor.matmul(slot[:, i * D:(i + 1) * D], xt[:, c, t * P:(t + 1) * P],
                                                            w[:, c, :], start=c == 0, stop=c == DC - 1)
                            give(key, last)

                    def head(buf, par, side, j, rows):
                        return buf[0:rows, par, side, j * T:(j + 1) * T]

                    def attention(a):
                        rows = STACK + PARTS * a
                        for item in SCHED[a]:
                            kind = item[0]
                            if kind == "num":
                                s, pair = item[2:]
                                g, i = divmod(s, NSTEP)
                                half, kb, lo, w = STEPS[i]
                                diagonal = lo == kb * P
                                if i == 0 and pair == 0:
                                    if a == 0:
                                        pe.wait_ge(stack_in[g % 2], 16 * 18 * (g // 2 + 1))
                                    else:
                                        pe.wait_ge(max_in[g % 2], 16 * (g // 2 + 1))
                                slot = take(item)
                                for k in range(2):
                                    j = 2 * pair + k
                                    dst = slot[:, k * HALF:k * HALF + w]
                                    last = nc.tensor.matmul(
                                        dst, head(turned, g % 2, 1, j, rows)[:, kb * P:(kb + 1) * P],
                                        head(turned, g % 2, 0, j, rows)[:, lo:lo + w], start=True, stop=not diagonal)
                                    if diagonal:
                                        last = nc.tensor.matmul(dst[:, 0:P], idb[:], mask_sb[:, 0, :],
                                                                start=False, stop=True)
                                give(item, last)
                            elif kind == "den":
                                g, j, qb = item[2:]
                                slot = take(item)
                                for half in range(2):
                                    cols = slice(half * HALF, (half + 1) * HALF)
                                    last = nc.tensor.matmul(slot[:, cols], head(plain, g % 2, 0, j, rows)[:, qb * P:(qb + 1) * P],
                                                            head(plain, g % 2, 1, j, rows)[:, cols], start=True, stop=True)
                                give(item, last)
                            elif kind == "max":
                                g, j, qb = item[2:]
                                if j == 0 and qb == 0:
                                    pe.wait_ge(stack_in[g % 2], 16 * (36 + 9 * (g // 2 + 1)))
                                slot = take(item)
                                w = (qb + 1) * P
                                lhs = head(turned, g % 2, 0, j, STACK)[:, qb * P:(qb + 1) * P]
                                for at in range(0, w, HALF):
                                    end = min(at + HALF, w)
                                    last = nc.tensor.matmul(slot[:, at:end], lhs, head(turned, g % 2, 1, j, STACK)[:, at:end],
                                                            start=True, stop=end < w)
                                last = nc.tensor.matmul(slot[:, w - P:w], idb[:], mask_sb[:, 1, :], start=False, stop=True)
                                give(item, last)
                            elif kind == "pv":
                                s = item[2]
                                g, i = divmod(s, NSTEP)
                                half, kb, lo, w = STEPS[i]
                                for pair in range(2):
                                    wait_drained(pe, ("num", a, s, pair))
                                n = 8 * a + 2 * g + half
                                if kb == 0 and n >= 1:
                                    pe.wait_ge(o_drained, n)
                                for j in range(GROUP):
                                    last = nc.tensor.matmul(
                                        o_bank[VC * j:VC * (j + 1), lo - half * HALF:HALF],
                                        vs[:, kb, GROUP * g + j, :], prob[:, s % 2, j * HALF:j * HALF + w],
                                        start=kb == 0, stop=closes(s), tile_position=(0, VC * j))
                                last.then_inc(pv_done, 1)
                            elif kind == "ot":
                                g, half = item[2:]
                                n = 8 * a + 2 * g + half
                                pe.wait_ge(o_drained, n + 1)
                                if BANK[item] >= 1:
                                    pe.wait_ge(t_drained, BANK[item])
                                for i in range(4):
                                    last = nc.tensor.transpose(t_bank[:, i * P:(i + 1) * P],
                                                               o_sb[:, n % 2, i * P:(i + 1) * P], idf[:])
                                last.then_inc(t_filled, 1)
                            elif kind == "mx":
                                g = item[2]
                                wait_drained(pe, ("max", a, g, GROUP - 1, TT - 1))
                                if BANK[item] >= 1:
                                    pe.wait_ge(t_drained, BANK[item])
                                nc.tensor.transpose(t_bank[0:GROUP * TT, 0:P], maxes[:, :], idf[:]).then_inc(t_filled, 1)

                    pe.wait_ge(normed, 1)
                    for c in range(DC):
                        transposes(("xt", 0, c), lambda t: xn[:, t, c * P:(c + 1) * P])
                    for c in range(DC):
                        wait_drained(pe, ("xt", 0, c))
                    project(0, 0)
                    project(0, 1)
                    for n in range(NU):
                        swap(0, n)
                        if n + 2 < NU:
                            project(0, n + 2)
                    values(0)
                    for h in range(2):
                        wait_drained(pe, ("v", 0, h))
                    attention(0)
                    pe.wait_ge(t_drained, BANK[("ot", 0, GROUPS - 1, 1)] + 1)
                    for c in range(DC):
                        transposes(("yt", 0, c), lambda t: xn[:, t, c * P:(c + 1) * P])
                    for c in range(DC):
                        wait_drained(pe, ("yt", 0, c))
                    out_project(0, wout_sb)
                    pe.wait_ge(normed, 2)
                    for c in range(DC):
                        transposes(("xt", 1, c), lambda t: xn[:, t, c * P:(c + 1) * P])
                    for c in range(DC):
                        wait_drained(pe, ("xt", 1, c))
                    slot = take(("lat",))
                    for t in range(TT):
                        for c in range(DC):
                            last = nc.tensor.matmul(slot[:, t * P:(t + 1) * P], xt[:, c, t * P:(t + 1) * P],
                                                    wdkv_sb[:, c, :], start=c == 0, stop=c == DC - 1)
                    give(("lat",), last)
                    project(1, 0)
                    project(1, 2)
                    wait_drained(pe, ("lat",))
                    transposes(("lt",), lambda t: latn[:, t * P:(t + 1) * P])
                    swap(1, 0)
                    swap(1, 1)
                    wait_drained(pe, ("lt",))
                    project(1, 1)
                    project(1, 3)
                    swap(1, 2)
                    swap(1, 3)
                    values(1)
                    for h in range(2):
                        wait_drained(pe, ("v", 1, h))
                    attention(1)
                    pe.wait_ge(t_drained, BANK[("ot", 1, GROUPS - 1, 1)] + 1)
                    for c in range(DC):
                        transposes(("yt", 1, c), lambda t: xn[:, t, c * P:(c + 1) * P])
                    for c in range(DC):
                        wait_drained(pe, ("yt", 1, c))
                    out_project(1, wo_sb)
                    pe.wait_ge(normed, 3)
                    for c in range(DC):
                        transposes(("xt", 2, c), lambda t: xn[:, t, c * P:(c + 1) * P])
                    for c in range(DC):
                        wait_drained(pe, ("xt", 2, c))
                    slot = take(("gate",))
                    for t in range(TT):
                        for c in range(DC):
                            last = nc.tensor.matmul(slot[:, t * EXPERTS:(t + 1) * EXPERTS], xt[:, c, t * P:(t + 1) * P],
                                                    gate_sb[:, c, :], start=c == 0, stop=c == DC - 1)
                    give(("gate",), last)
                    pe.wait_ge(onehot_ready, 1)
                    slot = take(("oht",))
                    for t in range(TT):
                        last = nc.tensor.transpose(slot[0:EXPERTS, t * P:(t + 1) * P], onehot[:, t, :], idf[:])
                    give(("oht",), last)
                    wait_drained(pe, ("oht",))
                    for h in range(2):
                        slot = take(("b2", h))
                        for i in range(4):
                            t = 4 * h + i
                            last = nc.tensor.matmul(slot[:, i * D:(i + 1) * D], oht[:, t * P:(t + 1) * P], b2_sb[:],
                                                    start=True, stop=True)
                        give(("b2", h), last)
                    for e in range(EXPERTS):
                        pe.wait_ge(w_landed[e % 2], 32 * (e // 2 + 1))
                        for h in range(2):
                            cols = slice(h * HALF, (h + 1) * HALF)
                            for n in range(HC // 2):
                                slot = take(("h", e, h, n))
                                for k in range(2):
                                    at = (2 * n + k) * P
                                    for c in range(DC):
                                        last = nc.tensor.matmul(slot[:, k * HALF:(k + 1) * HALF],
                                                                expert[e % 2][:, c * HID + at:c * HID + at + P],
                                                                xt[:, c, cols], start=c == 0, stop=c == DC - 1)
                                give(("h", e, h, n), last)
                        for h in range(2):
                            wait_drained(pe, ("h", e, h, HC // 2 - 1))
                            slot = take(("y", e, h))
                            for i in range(4):
                                for n in range(HC):
                                    at = DC * HID + n * D
                                    last = nc.tensor.matmul(slot[:, i * D:(i + 1) * D],
                                                            hidden[h][:, n * HALF + i * P:n * HALF + (i + 1) * P],
                                                            expert[e % 2][:, at:at + D], start=n == 0, stop=n == HC - 1)
                            give(("y", e, h), last)

                @block.scalar
                def _(act):
                    def roots(n):
                        act.wait_ge(var_ready, n)
                        nc.scalar.activation(t8[:, 1, :], t8[:, 0, :], ACT.Sqrt).then_inc(std_ready, 1)

                    def evacuate_q(a, n):
                        u = ORDER[a][n]
                        if n >= 2:
                            filled(act, ("swap", a, ORDER[a][n - 2]))
                            act.wait_ge(cos_done, NU * a + n - 1)
                            if a == 0:
                                act.wait_ge(split_done, jobs_before(0, n - 2, 0) + 1)
                        slot = filled(act, ("proj", a, u))
                        nc.scalar.activation(qs[n % 2], slot[:], ACT.Copy).then_inc(drained(("proj", a, u)), 1)

                    def evacuate_v(a):
                        for h in range(2):
                            slot = filled(act, ("v", a, h))
                            nc.scalar.activation(vs[:, 4 * h:4 * h + 4, :, 0:HD],
                                                 slot[:].rearrange("p (t h d) -> p t h d", t=4, h=HEADS),
                                                 ACT.Copy).then_inc(drained(("v", a, h)), 1)

                    def attention(a):
                        for item in SCHED[a]:
                            if item[0] == "num":
                                s, pair = item[2:]
                                w = STEPS[s % NSTEP][3]
                                if pair == 0 and s >= 2:
                                    act.wait_ge(pv_done, NALL * a + s - 1)
                                slot = filled(act, item)
                                dst = prob[:, s % 2, 2 * pair * HALF:(2 * pair + 2) * HALF]
                                nc.scalar.activation(dst.rearrange("p (h n) -> p h n", h=2)[:, :, 0:w],
                                                     slot[:].rearrange("p (h n) -> p h n", h=2)[:, :, 0:w],
                                                     ACT.Exp, scale=SCALE).then_inc(drained(item), 1)
                            elif item[0] == "den":
                                g, j, qb = item[2:]
                                slot = filled(act, item)
                                h = GROUP * g + j
                                nc.scalar.activation(slot[:], slot[:], ACT.Exp, scale=SCALE,
                                                     accum_out=sums[:, qb, h:h + 1]).then_inc(drained(item), 1)

                    roots(1)
                    slot = filled(act, ("xt", 0, 0))
                    nc.scalar.activation(xt[:, 0, :], slot[:], ACT.Copy).then_inc(drained(("xt", 0, 0)), 1)
                    for n in range(NU):
                        evacuate_q(0, n)
                    evacuate_v(0)
                    attention(0)
                    slot = filled(act, ("yt", 0, 0))
                    nc.scalar.activation(xt[:, 0, :], slot[:], ACT.Copy).then_inc(drained(("yt", 0, 0)), 1)
                    roots(2)
                    roots(3)
                    slot = filled(act, ("xt", 1, 0))
                    nc.scalar.activation(xt[:, 0, :], slot[:], ACT.Copy,
                                         scale=norms_sb[:, 0, 0:1]).then_inc(drained(("xt", 1, 0)), 1)
                    roots(4)
                    for n in range(NU):
                        evacuate_q(1, n)
                    evacuate_v(1)
                    attention(1)
                    slot = filled(act, ("yt", 1, 0))
                    nc.scalar.activation(xt[:, 0, :], slot[:], ACT.Copy).then_inc(drained(("yt", 1, 0)), 1)
                    roots(5)
                    slot = filled(act, ("xt", 2, 0))
                    nc.scalar.activation(xt[:, 0, :], slot[:], ACT.Copy,
                                         scale=norms_sb[:, 1, 0:1]).then_inc(drained(("xt", 2, 0)), 1)
                    for e in range(EXPERTS):
                        for h in range(2):
                            if e >= 1:
                                filled(act, ("y", e - 1, h))
                            for n in range(HC // 2):
                                slot = filled(act, ("h", e, h, n))
                                for k in range(2):
                                    at = 2 * n + k
                                    ins = nc.scalar.activation(hidden[h][:, at * HALF:(at + 1) * HALF],
                                                               slot[:, k * HALF:(k + 1) * HALF], ACT.Relu,
                                                               bias=b1_sb[:, e, at:at + 1])
                                ins.then_inc(drained(("h", e, h, n)), 1)

                @block.gpsimd
                def _(pool):
                    pool.wait_ge(normed, 1)
                    nc.gpsimd.tensor_tensor(xs[:], xs[:], bout_sb[:].unsqueeze(1).to_broadcast([P, TT, D]),
                                            ALU.add).then_inc(bias_added, 1)

                    def cosines(a, n):
                        u = ORDER[a][n]
                        wait_drained(pool, ("proj", a, u))
                        if NU * a + n >= 1:
                            pool.wait_ge(rot_done, NU * a + n)
                        nc.gpsimd.tensor_tensor(cosq, qs[n % 2], cos_sb[:, a, :], ALU.mult).then_inc(cos_done, 1)

                    for n in range(NU):
                        cosines(0, n)
                    for n in range(NU):
                        cosines(1, n)

                @block.vector
                def _(dve):
                    steps = [0]

                    def link(ins):
                        steps[0] += 1
                        ins.then_inc(v_step, 1)
                        dve.wait_ge(v_step, steps[0])

                    def token_stats(src):
                        for t in range(TT):
                            ins = nc.vector.bn_stats(stats[:, t, :], src(t))
                        link(ins)
                        for t in range(TT):
                            ins = nc.vector.bn_aggr(mv[:, t, :], stats[:, t, :])
                        link(ins)

                    def inverse_root(n, src, eps, dst):
                        nc.vector.tensor_scalar(t8[:, 0, :], src, eps, None, ALU.add).then_inc(var_ready, 1)
                        dve.wait_ge(std_ready, n)
                        link(nc.vector.reciprocal(dst, t8[:, 1, :]))

                    def split(a, n, rotated, src):
                        job = jobs_before(a, n, rotated)
                        par = job % 2
                        if job >= 2:
                            dve.wait_ge(parts_out[par], 16 * PARTS * (job // 2))
                        link(nc.vector.tensor_copy(parts[:, par, 0, :], src))
                        link(nc.vector.tensor_tensor(rest[:], src, parts[:, par, 0, :], ALU.subtract))
                        link(nc.vector.tensor_copy(parts[:, par, 1, :], rest[:]))
                        nc.vector.tensor_tensor(parts[:, par, 2, :], rest[:], parts[:, par, 1, :],
                                                ALU.subtract).then_inc(split_done, 1)
                        dve.wait_ge(split_done, job + 1)

                    def plain_parts(n):
                        wait_drained(dve, ("proj", 0, ORDER[0][n]))
                        split(0, n, 0, qs[n % 2])

                    def rotate(a, n):
                        key = ("swap", a, ORDER[a][n])
                        slot = filled(dve, key)
                        nc.vector.tensor_tensor(rot, slot[:], sin_sb[:, a, :], ALU.mult).then_inc(drained(key), 1)
                        wait_drained(dve, key)
                        dve.wait_ge(cos_done, NU * a + n + 1)
                        nc.vector.tensor_tensor(rot, rot, cosq, ALU.add).then_inc(rot_done, 1)
                        dve.wait_ge(rot_done, NU * a + n + 1)
                        split(a, n, 1, rot)

                    def attention(a):
                        for item in SCHED[a]:
                            if item[0] == "max":
                                g, j, qb = item[2:]
                                slot = filled(dve, item)
                                if g >= 1 and j == 0 and qb == 0:
                                    dve.wait_ge(t_filled, BANK[("mx", a, g - 1)] + 1)
                                at = j * TT + qb
                                nc.vector.reduce_max(maxes[:, at:at + 1], slot[:, 0:(qb + 1) * P],
                                                     AX_X).then_inc(drained(item), 1)
                            elif item[0] == "mx":
                                g = item[2]
                                dve.wait_ge(t_filled, BANK[item] + 1)
                                if g >= 1:
                                    dve.wait_ge(max_out, 16 * PARTS * g)
                                nc.vector.tensor_scalar(mrow[:, 0, :], t_bank[0:GROUP * TT, 0:P], -1.0, None,
                                                        ALU.mult).then_inc(t_drained, 1)
                                dve.wait_ge(t_drained, BANK[item] + 1)
                                link(nc.vector.tensor_copy(mpart[:, 0, :], mrow[:, 0, :]))
                                link(nc.vector.tensor_tensor(mrow[:, 1, :], mrow[:, 0, :], mpart[:, 0, :], ALU.subtract))
                                link(nc.vector.tensor_copy(mpart[:, 1, :], mrow[:, 1, :]))
                                nc.vector.tensor_tensor(mpart[:, 2, :], mrow[:, 1, :], mpart[:, 1, :],
                                                        ALU.subtract).then_inc(max_split, 1)
                            elif item[0] == "pv" and closes(item[2]):
                                n = HALVES[item]
                                dve.wait_ge(pv_done, NALL * a + item[2] + 1)
                                nc.vector.tensor_copy(o_sb[:, n % 2, :], o_bank[:]).then_inc(o_drained, 1)
                            elif item[0] == "ot":
                                g, half = item[2:]
                                rc = recip[:].rearrange("p (t h) -> p t h", t=4)
                                turned_o = t_bank[:].rearrange("p (t h c) -> p t h c", t=4, h=GROUP)
                                dve.wait_ge(t_filled, BANK[item] + 1)
                                if a == 0:
                                    wait_drained(dve, ("den", 0, g, GROUP - 1, 4 * half + 3))
                                    link(nc.vector.reciprocal(rc, sums[:, 4 * half:4 * half + 4, GROUP * g:GROUP * (g + 1)]))
                                else:
                                    link(nc.vector.reciprocal(rc.unsqueeze(3), turned_o[:, :, :, HD:HD + 1]))
                                dst = xn[:, 4 * half:4 * half + 4, :].rearrange("p t (h d) -> p t h d", h=HEADS)
                                nc.vector.tensor_tensor(dst[:, :, GROUP * g:GROUP * (g + 1), :], turned_o[:, :, :, 0:HD],
                                                        rc.unsqueeze(3).to_broadcast([P, 4, GROUP, HD]),
                                                        ALU.mult).then_inc(t_drained, 1)

                    def residual(dst, key, h):
                        slot = filled(dve, key)
                        part = dst[:, 4 * h:4 * h + 4, :].rearrange("p t d -> p (t d)")
                        nc.vector.tensor_tensor(part, slot[:], part, ALU.add).then_inc(drained(key), 1)
                        wait_drained(dve, key)

                    dve.wait_ge(x_landed, 16)
                    token_stats(lambda t: xs[:, t, :])
                    inverse_root(1, mv[:, :, 1], 1e-5, t8[:, 2, :])
                    for t in range(TT):
                        ins = nc.vector.tensor_scalar(xn[:, t, :], xs[:, t, :], mv[:, t, 0:1], t8[:, 2, t:t + 1],
                                                      ALU.subtract, ALU.mult)
                    ins.then_inc(normed, 1)
                    slot = filled(dve, ("xt", 0, 1))
                    nc.vector.tensor_copy(xt[:, 1, :], slot[:]).then_inc(drained(("xt", 0, 1)), 1)
                    for n in range(NU):
                        plain_parts(n)
                        rotate(0, n)
                    attention(0)
                    slot = filled(dve, ("yt", 0, 1))
                    nc.vector.tensor_copy(xt[:, 1, :], slot[:]).then_inc(drained(("yt", 0, 1)), 1)
                    dve.wait_ge(bias_added, 1)
                    for h in range(2):
                        residual(xs, ("op", 0, h), h)
                    token_stats(lambda t: xs[:, t, :])
                    inverse_root(2, mv[:, :, 1], 1e-5, t8[:, 2, :])
                    link(nc.vector.tensor_tensor(t8[:, 3, :], mv[:, :, 1], t8[:, 2, :], ALU.mult))
                    link(nc.vector.tensor_tensor(t8[:, 3, :], t8[:, 3, :], t8[:, 2, :], ALU.mult))
                    inverse_root(3, t8[:, 3, :], 1e-6, t8[:, 4, :])
                    for t in range(TT):
                        ins = nc.vector.tensor_scalar(zs[:, t, :], xs[:, t, :], mv[:, t, 0:1], t8[:, 2, t:t + 1],
                                                      ALU.subtract, ALU.mult)
                    link(ins)
                    for t in range(TT):
                        ins = nc.vector.tensor_scalar(xn[:, t, :], zs[:, t, :], t8[:, 4, t:t + 1], None, ALU.mult)
                    ins.then_inc(normed, 1)
                    slot = filled(dve, ("xt", 1, 1))
                    nc.vector.tensor_scalar(xt[:, 1, :], slot[:], norms_sb[:, 0, 1:2], None,
                                            ALU.mult).then_inc(drained(("xt", 1, 1)), 1)
                    slot = filled(dve, ("lat",))
                    lat_slot = slot
                    token_stats(lambda t: lat_slot[:, t * P:(t + 1) * P])
                    inverse_root(4, mv[:, :, 1], 1e-5, t8[:, 2, :])
                    for t in range(TT):
                        ins = nc.vector.tensor_scalar(latn[:, t * P:(t + 1) * P], slot[:, t * P:(t + 1) * P],
                                                      mv[:, t, 0:1], t8[:, 2, t:t + 1], ALU.subtract, ALU.mult)
                    ins.then_inc(drained(("lat",)), 1)
                    wait_drained(dve, ("lat",))
                    slot = filled(dve, ("lt",))
                    nc.vector.tensor_scalar(latt, slot[:], ln_sb[:, 0:1], ln_sb[:, 1:2], ALU.mult,
                                            ALU.add).then_inc(drained(("lt",)), 1)
                    for n in range(NU):
                        rotate(1, n)
                    attention(1)
                    slot = filled(dve, ("yt", 1, 1))
                    nc.vector.tensor_copy(xt[:, 1, :], slot[:]).then_inc(drained(("yt", 1, 1)), 1)
                    for h in range(2):
                        residual(zs, ("op", 1, h), h)
                    token_stats(lambda t: zs[:, t, :])
                    link(nc.vector.tensor_tensor(t8[:, 3, :], mv[:, :, 0], mv[:, :, 0], ALU.mult))
                    link(nc.vector.tensor_tensor(t8[:, 3, :], t8[:, 3, :], mv[:, :, 1], ALU.add))
                    inverse_root(5, t8[:, 3, :], 1e-6, t8[:, 4, :])
                    for t in range(TT):
                        ins = nc.vector.tensor_scalar(xn[:, t, :], zs[:, t, :], t8[:, 4, t:t + 1], None, ALU.mult)
                    ins.then_inc(normed, 1)
                    nc.vector.tensor_tensor(xs[:], xs[:], zs[:], ALU.add).then_inc(xr_done, 1)
                    slot = filled(dve, ("xt", 2, 1))
                    nc.vector.tensor_scalar(xt[:, 1, :], slot[:], norms_sb[:, 1, 1:2], None,
                                            ALU.mult).then_inc(drained(("xt", 2, 1)), 1)
                    slot = filled(dve, ("gate",))
                    nc.vector.tensor_tensor(logits[:], slot[:, 0:TT * EXPERTS].rearrange("p (t e) -> p t e", e=EXPERTS),
                                            gate_b_sb[:].unsqueeze(1).to_broadcast([P, TT, EXPERTS]),
                                            ALU.add).then_inc(drained(("gate",)), 1)
                    wait_drained(dve, ("gate",))
                    link(nc.vector.reduce_max(top[:], logits[:], AX_X))
                    link(nc.vector.tensor_tensor(onehot[:], logits[:], top[:].unsqueeze(2).to_broadcast([P, TT, EXPERTS]),
                                                 ALU.is_ge))
                    link(nc.vector.tensor_copy(top[:], onehot[:, :, 0]))
                    for e in range(1, EXPERTS):
                        ins = nc.vector.tensor_tensor(onehot[:, :, e], onehot[:, :, e], top[:], ALU.is_gt)
                        if e < EXPERTS - 1:
                            link(ins)
                            link(nc.vector.tensor_tensor(top[:], top[:], onehot[:, :, e], ALU.max))
                    ins.then_inc(onehot_ready, 1)
                    dve.wait_ge(onehot_ready, 1)
                    slot = filled(dve, ("oht",))
                    nc.vector.tensor_copy(oht[:], slot[0:EXPERTS, :]).then_inc(drained(("oht",)), 1)
                    dve.wait_ge(xr_done, 1)
                    for h in range(2):
                        residual(xs, ("b2", h), h)
                    for e in range(EXPERTS):
                        for h in range(2):
                            slot = filled(dve, ("y", e, h))
                            for i in range(4):
                                t = 4 * h + i
                                ins = nc.vector.scalar_tensor_tensor(
                                    out=xs[:, t, :], in0=slot[:, i * D:(i + 1) * D], scalar=onehot[:, t, e:e + 1],
                                    in1=xs[:, t, :], op0=ALU.mult, op1=ALU.add)
                                if i < 3:
                                    continue
                                ins.then_inc(drained(("y", e, h)), 1)
                            wait_drained(dve, ("y", e, h))

            for s in in_loop:
                nc.sync.sem_clear(s)
            nc.all_engine_barrier()


def kernel(L0_attn_x, L0_attn_w_qkv, L0_attn_w_out, L0_attn_b_out, L0_ffn_norm1_w, L0_ffn_norm2_w, L0_ffn_Wq,
           L0_ffn_Wdkv, L0_ffn_Wuk, L0_ffn_Wuv, L0_ffn_Wo, L0_ffn_ln_g, L0_ffn_ln_b, L0_ffn_gate_w, L0_ffn_gate_b,
           L0_ffn_W1, L0_ffn_b1, L0_ffn_W2, L0_ffn_b2):
    import ml_dtypes
    import numpy as np
    import concourse.bacc as bacc
    from concourse.bass_utils import run_bass_kernel_spmd

    def chunked(w):
        w = np.asarray(w)
        return np.ascontiguousarray(w.T.reshape(-1, P, w.shape[0]).transpose(1, 0, 2))

    def columns(v):
        v = np.asarray(v)
        v = v.reshape(*v.shape[:-1], -1, P)
        return np.ascontiguousarray(np.moveaxis(v, -1, 0))

    def every_partition(v):
        return np.ascontiguousarray(np.broadcast_to(np.asarray(v), (P, np.asarray(v).shape[-1])))

    f32 = np.float32
    half = HD // 2
    pos = np.arange(T, dtype=f32)
    i = np.arange(half, dtype=f32)
    theta0 = (10000.0 ** ((-2.0 * (i - 1.0) / HD).astype(np.float64))).astype(f32)
    theta1 = (1.0 / (10000.0 ** (np.arange(half) / half)).astype(f32)).astype(f32)
    row = np.arange(P)
    d = row % HD
    angle0 = (pos[None, :] * theta0[d // 2][:, None]).astype(np.float64)
    angle1 = (pos[None, :] * theta1[d % half][:, None]).astype(np.float64)
    sign0 = np.where(d % 2 == 0, 1.0, -1.0)[:, None]
    sign1 = np.where(d < half, -1.0, 1.0)[:, None]
    cos = np.stack([np.cos(angle0), np.cos(angle1)], 1).astype(f32)
    sin = np.stack([np.sin(angle0) * sign0, np.sin(angle1) * sign1], 1).astype(f32)
    perm = np.zeros((P, 2, P), f32)
    perm[row ^ 1, 0, row] = 1
    perm[row ^ half, 1, row] = 1
    ident = np.eye(P, dtype=f32)
    at = np.arange(P)
    keys_first = np.where(at[:, None] > at[None, :], MASKED, 0.0)
    mask = np.stack([keys_first, keys_first.T], 1)

    W1, W2 = np.asarray(L0_ffn_W1), np.asarray(L0_ffn_W2)
    arrays = {
        "x": np.asarray(L0_attn_x),
        "wqkv": chunked(L0_attn_w_qkv), "wout": chunked(L0_attn_w_out), "bout": every_partition(L0_attn_b_out),
        "norms": columns(np.stack([np.asarray(L0_ffn_norm1_w), np.asarray(L0_ffn_norm2_w)])),
        "wq": chunked(L0_ffn_Wq), "wdkv": chunked(L0_ffn_Wdkv), "wuk": chunked(L0_ffn_Wuk)[:, 0],
        "wuv": chunked(L0_ffn_Wuv)[:, 0], "wo": chunked(L0_ffn_Wo),
        "lnp": np.ascontiguousarray(np.stack([np.asarray(L0_ffn_ln_g), np.asarray(L0_ffn_ln_b)], 1)),
        "gate": chunked(L0_ffn_gate_w), "gate_b": every_partition(L0_ffn_gate_b),
        "w1": np.stack([chunked(W1[e]).reshape(P, -1) for e in range(EXPERTS)]),
        "b1": columns(L0_ffn_b1),
        "w2": np.stack([chunked(W2[e]).reshape(P, -1) for e in range(EXPERTS)]),
        "b2": np.asarray(L0_ffn_b2),
        "cos": cos, "sin": sin, "perm": perm,
        "ident_f": ident, "ident_b": ident.astype(ml_dtypes.bfloat16), "mask_b": mask.astype(ml_dtypes.bfloat16),
    }
    nc = bacc.Bacc("TRN2", target_bir_lowering=False, num_devices=1)
    args = {}
    for name, a in arrays.items():
        arrays[name] = a = np.ascontiguousarray(a)
        args[name] = nc.dram_tensor("in_" + name, a.shape, mybir.dt.from_np(a.dtype), kind="ExternalInput").ap()
    out = nc.dram_tensor("out_x", (B, T, D), F32, kind="ExternalOutput").ap()
    build(nc, **args, out=out)
    r = run_bass_kernel_spmd(nc, [{"in_" + n: a for n, a in arrays.items()}], core_ids=[0])
    return r.results[0]["out_x"]
```

```python
from contextlib import ExitStack

import concourse.bass as bass
from concourse import mybir

P = 128
D = 256
HEADS, HD = 16, 16
LAT = 128
EXPERTS, HID = 4, 1024
B, T = 8, 1024
TT = T // P
DC = D // P
HC = HID // P
HALF = 512
GROUP = 4
GROUPS = HEADS // GROUP
VC = P // GROUP
PARTS = 3
TERMS = [(0, 0), (1, 0), (2, 0), (0, 1), (1, 1), (0, 2)]
STACK = len(TERMS) * HD
SCALE = 1.0 / 4.0
MASKED = -1e30
SLOTS = 3

UNROLL = 17
TILES = -(-(B * TT + EXPERTS - 1) // UNROLL) * UNROLL
GATHERED = 4

F32 = mybir.dt.float32
I32 = mybir.dt.int32
U32 = mybir.dt.uint32
BF16 = mybir.dt.bfloat16
ALU = mybir.AluOpType
ACT = mybir.ActivationFunctionType
AX_X = mybir.AxisListType.X

STEPS = []
for _h in range(2):
    for _kb in range(4 * _h + 4):
        _lo = max(_kb * P, _h * HALF)
        STEPS.append((_h, _kb, _lo, (_h + 1) * HALF - _lo))
NSTEP = len(STEPS)
NALL = GROUPS * NSTEP


def attention_schedule(a):
    items = []
    if a == 1:
        items += [("max", a, 0, j, qb) for j in range(GROUP) for qb in range(TT)]
        items.append(("mx", a, 0))
    for s in range(NALL):
        g, i = divmod(s, NSTEP)
        half = STEPS[i][0]
        items += [("num", a, s, pair) for pair in range(2)]
        if a == 0:
            per = 16 // (4 * half + 4)
            at = per * (i - 4 * half)
            items += [("den", a, g, n % GROUP, 4 * half + n // GROUP) for n in range(at, at + per)]
        if s >= 1:
            items.append(("pv", a, s - 1))
        if s >= 2 and closes(s - 2):
            items.append(("ot", a, (s - 2) // NSTEP, STEPS[(s - 2) % NSTEP][0]))
        if a == 1 and g + 1 < GROUPS and 2 <= i < 10:
            items += [("max", a, g + 1, n // TT, n % TT) for n in range(4 * (i - 2), 4 * (i - 1))]
        elif a == 1 and g + 1 < GROUPS and i == 10:
            items.append(("mx", a, g + 1))
    items.append(("pv", a, NALL - 1))
    items.append(("ot", a, GROUPS - 1, 1))
    return items


def closes(s):
    i = s % NSTEP
    return i == NSTEP - 1 or STEPS[i + 1][0] != STEPS[i][0]


UNITS = [("q", 0), ("k", 0), ("q", 1), ("k", 1)]
NU = len(UNITS)

SCHED = [attention_schedule(0), attention_schedule(1)]


def plan_slots():
    uses = [("xt", 0, c) for c in range(DC)]
    uses += [("proj", 0, 0), ("proj", 0, 1)]
    for u in range(NU):
        uses.append(("swap", 0, u))
        if u + 2 < NU:
            uses.append(("proj", 0, u + 2))
    uses += [("v", 0, h) for h in range(2)]
    uses += [x for x in SCHED[0] if x[0] in ("num", "den")]
    uses += [("yt", 0, c) for c in range(DC)] + [("op", 0, h) for h in range(2)]
    uses += [("xt", 1, c) for c in range(DC)]
    uses += [("lat",), ("proj", 1, 0), ("proj", 1, 2), ("lt",), ("swap", 1, 0), ("swap", 1, 2)]
    uses += [("proj", 1, 1), ("proj", 1, 3), ("swap", 1, 1), ("swap", 1, 3)]
    uses += [("v", 1, h) for h in range(2)]
    uses += [x for x in SCHED[1] if x[0] in ("num", "max")]
    uses += [("yt", 1, c) for c in range(DC)] + [("op", 1, h) for h in range(2)]
    uses += [("xt", 2, c) for c in range(DC)]
    uses += [("gate",), ("oht",)] + [("b2", h) for h in range(2)]
    return {key: n for n, key in enumerate(uses)}


ORDER = [[0, 1, 2, 3], [0, 2, 1, 3]]
SLOT = plan_slots()
BANK = {x: n for n, x in enumerate(x for a in range(2) for x in SCHED[a] if x[0] in ("ot", "mx"))}
HALVES = {x: n for n, x in enumerate(("pv", a, s) for a in range(2) for s in range(NALL) if closes(s))}


def jobs_before(a, n, rotated):
    return 2 * n + rotated if a == 0 else 2 * NU + n


def build(nc, x, wqkv, wout, bout, norms, wq, wdkv, wuk, wuv, wo, lnp, gate, gate_b, w1, b1, w2, b2,
          cos, sin, perm, ident_f, ident_b, mask_b, before, starts, tile_ids, token_ids, no_token, zero_row, out):
    rows = nc.dram_tensor("rows", (B * T + 1, 2 * D), F32, kind="Internal").ap()
    chosen = nc.dram_tensor("chosen", (B, P, TT, EXPERTS), F32, kind="Internal").ap()
    build_sequences(nc, x, wqkv, wout, bout, norms, wq, wdkv, wuk, wuv, wo, lnp, gate, gate_b, b2,
                    cos, sin, perm, ident_f, ident_b, mask_b, rows, chosen)
    build_experts(nc, rows, chosen, norms, w1, b1, w2, ident_f, before, starts, tile_ids, token_ids, no_token,
                  zero_row, out)


def build_sequences(nc, x, wqkv, wout, bout, norms, wq, wdkv, wuk, wuv, wo, lnp, gate, gate_b, b2,
                    cos, sin, perm, ident_f, ident_b, mask_b, rows, chosen):
    scratch = nc.dram_tensor("head_parts", (6, HEADS, PARTS, HD, T), BF16, kind="Internal").ap()
    max_scratch = nc.dram_tensor("max_parts", (2, PARTS, GROUP, T), BF16, kind="Internal").ap()

    with ExitStack() as ctx:
        def sb(name, shape, dt=F32):
            return ctx.enter_context(nc.sbuf_tensor(name, shape, dt))

        def sem(name):
            return ctx.enter_context(nc.semaphore(name))

        slots = [ctx.enter_context(nc.psum_tensor(f"slot{i}", [P, 2 * HALF], F32)) for i in range(SLOTS)]
        o_bank = ctx.enter_context(nc.psum_tensor("o_bank", [P, HALF], F32))
        t_bank = ctx.enter_context(nc.psum_tensor("t_bank", [P, HALF], F32))

        wqkv_sb = sb("wqkv_sb", [P, DC, 3 * D])
        wout_sb = sb("wout_sb", [P, DC, D])
        wq_sb = sb("wq_sb", [P, DC, D])
        wdkv_sb = sb("wdkv_sb", [P, DC, LAT])
        wuk_sb = sb("wuk_sb", [P, D])
        wuv_sb = sb("wuv_sb", [P, D])
        wo_sb = sb("wo_sb", [P, DC, D])
        gate_sb = sb("gate_sb", [P, DC, EXPERTS])
        bout_sb = sb("bout_sb", [P, D])
        gate_b_sb = sb("gate_b_sb", [P, EXPERTS])
        norms_sb = sb("norms_sb", [P, 2, DC])
        ln_sb = sb("ln_sb", [P, 2])
        b2_sb = sb("b2_sb", [EXPERTS, D])
        cos_sb = sb("cos_sb", [P, 2, T])
        sin_sb = sb("sin_sb", [P, 2, T])
        perm_sb = sb("perm_sb", [P, 2, P])
        idf = sb("idf", [P, P])
        idb = sb("idb", [P, P], BF16)
        mask_sb = sb("mask_sb", [P, 2, P], BF16)

        xs = sb("xs", [P, TT, D])
        xn = sb("xn", [P, TT, D])
        zs = sb("zs", [P, TT, D])
        xt = sb("xt", [P, DC, T])
        tmp = sb("tmp", [P, 4 * T])
        qs = [tmp[:, 0:T], tmp[:, T:2 * T]]
        cosq = tmp[:, 2 * T:3 * T]
        rot = tmp[:, 3 * T:4 * T]
        rest = sb("rest", [P, T])
        parts = sb("parts", [P, 2, PARTS, T], BF16)
        vs = sb("vs", [P, TT, HEADS, VC])
        plain = sb("plain", [P, 2, 2, GROUP * T], BF16)
        turned = sb("turned", [P, 2, 2, GROUP * T], BF16)
        prob = sb("prob", [P, 2, GROUP * HALF])
        o_sb = sb("o_sb", [P, 2, HALF])
        sums = sb("sums", [P, TT, HEADS])
        recip = sb("recip", [P, 16])
        stats = sb("stats", [P, TT, 6])
        mv = sb("mv", [P, TT, 2])
        t8 = sb("t8", [P, 6, TT])
        latn, latt = xn[:, :, :].rearrange("p t d -> p (t d)")[:, 0:T], xn[:, :, :].rearrange("p t d -> p (t d)")[:, T:2 * T]
        maxes = sb("maxes", [P, GROUP * TT])
        mrow = sb("mrow", [GROUP * TT, 2, P])
        mpart = sb("mpart", [GROUP * TT, PARTS, P], BF16)
        logits = sb("logits", [P, TT, EXPERTS])
        top = sb("top", [P, TT])
        onehot = sb("onehot", [P, TT, EXPERTS])
        oht = sb("oht", [EXPERTS, T])

        s_const = sem("s_const")
        values_padded = sem("values_padded")
        ones_written = sem("ones_written")
        slot_filled = [sem(f"slot_filled{i}") for i in range(SLOTS)]
        slot_drained = [sem(f"slot_drained{i}") for i in range(SLOTS)]
        x_landed = sem("x_landed")
        v_step = sem("v_step")
        var_ready = sem("var_ready")
        std_ready = sem("std_ready")
        normed = sem("normed")
        bias_added = sem("bias_added")
        cos_done = sem("cos_done")
        rot_done = sem("rot_done")
        split_done = sem("split_done")
        onehot_ready = sem("onehot_ready")
        parts_out = [sem(f"parts_out{i}") for i in range(2)]
        stack_in = [sem(f"stack_in{i}") for i in range(2)]
        pv_done = sem("pv_done")
        o_filled = sem("o_filled")
        o_drained = sem("o_drained")
        t_filled = sem("t_filled")
        t_drained = sem("t_drained")
        max_split = sem("max_split")
        max_out = sem("max_out")
        max_in = [sem(f"max_in{i}") for i in range(2)]
        xr_done = sem("xr_done")
        out_done = sem("out_done")
        in_loop = ([x_landed, v_step, var_ready, std_ready, normed, bias_added, cos_done,
                    rot_done, split_done, onehot_ready, pv_done, o_filled, o_drained, t_filled, t_drained,
                    max_split, max_out, xr_done, out_done] + slot_filled + slot_drained
                   + parts_out + stack_in + max_in)

        def filled(eng, key):
            n = SLOT[key]
            eng.wait_ge(slot_filled[n % SLOTS], n // SLOTS + 1)
            return slots[n % SLOTS]

        def wait_drained(eng, key):
            n = SLOT[key]
            eng.wait_ge(slot_drained[n % SLOTS], n // SLOTS + 1)

        def drained(key):
            return slot_drained[SLOT[key] % SLOTS]

        consts = [(wqkv_sb, wqkv), (wout_sb, wout), (wq_sb, wq), (wdkv_sb, wdkv), (wuk_sb, wuk), (wuv_sb, wuv),
                  (wo_sb, wo), (gate_sb, gate), (bout_sb, bout), (gate_b_sb, gate_b), (norms_sb, norms),
                  (ln_sb, lnp), (b2_sb, b2), (cos_sb, cos), (sin_sb, sin), (perm_sb, perm),
                  (idf, ident_f), (idb, ident_b), (mask_sb, mask_b)]
        with nc.Block(no_gpsimd_drain=True) as block:
            @block.sync
            def _(sp):
                for dst, src in consts:
                    sp.dma_start(dst[:], src).then_inc(s_const, 16)
                sp.wait_ge(s_const, 16 * len(consts))

            @block.vector
            def _(dve):
                nc.vector.memset(vs[:], 0.0).then_inc(values_padded, 1)
                dve.wait_ge(values_padded, 1)
                nc.vector.memset(vs[:, :, :, HD:HD + 1], 1.0).then_inc(values_padded, 1)
                dve.wait_ge(values_padded, 2)

            @block.gpsimd
            def _(pool):
                for par in range(2):
                    nc.gpsimd.memset(turned[STACK:STACK + PARTS, par, 1, :], 1.0).then_inc(ones_written, 1)
                pool.wait_ge(ones_written, 2)

        with nc.Fori(0, B, 1) as b:
            with nc.Block(no_gpsimd_drain=True) as block:
                x_b = x[bass.ds(b, 1)].rearrange("b (t p) d -> p (b t) d", p=P)
                rows_b = rows[0:B * T].rearrange("(b t p) c -> b p t c", b=B, p=P)[bass.ds(b, 1)].rearrange("b p t c -> (b p) t c")
                chosen_b = chosen[bass.ds(b, 1)].rearrange("b p t e -> (b p) t e")

                @block.sync
                def _(sp):
                    sp.dma_start(xs[:], x_b).then_inc(x_landed, 16)

                    def store_parts(a, n, rotated):
                        tensor, blk = UNITS[ORDER[a][n]]
                        job = jobs_before(a, n, rotated)
                        row = 4 * a + 2 * rotated * (1 - a) + (tensor == "k")
                        sp.wait_ge(split_done, job + 1)
                        for t in range(PARTS):
                            sp.dma_start(scratch[row, 8 * blk:8 * blk + 8, t],
                                         parts[:, job % 2, t, :]).then_inc(parts_out[job % 2], 16)

                    def load_stack(dst, row, g, side, par):
                        h0 = GROUP * g
                        at = 0
                        for term in ([[0, 1, 2], [0, 1], [0]] if side == 0 else [[0], [0], [0], [1], [1], [2]]):
                            n = len(term) * HD
                            src = scratch[row, h0:h0 + GROUP, term[0]:term[-1] + 1].rearrange("h t d n -> (t d) h n")
                            sp.dma_start(dst[at:at + n, :].rearrange("p (h n) -> p h n", h=GROUP),
                                         src).then_inc(stack_in[par], 16)
                            at += n

                    def load_group(a, g):
                        par = g % 2
                        if a == 0:
                            if g >= 2:
                                sp.wait_ge(pv_done, NSTEP * (g - 1))
                            for par_out in range(2):
                                sp.wait_ge(parts_out[par_out], 16 * PARTS * (2 if g < 2 else 4))
                            for side in range(2):
                                load_stack(plain[:, par, side], side, g, side, par)
                                load_stack(turned[:, par, side], 2 + side, g, side, par)
                        else:
                            sp.wait_ge(pv_done, NSTEP * (GROUPS + g - 1))
                            for par_out in range(2):
                                sp.wait_ge(parts_out[par_out], 16 * PARTS * 6)
                            for side in range(2):
                                load_stack(turned[:, par, side], 4 + side, g, side, par)

                    for n in range(2):
                        store_parts(0, n, 0)
                        store_parts(0, n, 1)
                    load_group(0, 0)
                    load_group(0, 1)
                    for n in range(2, 4):
                        store_parts(0, n, 0)
                        store_parts(0, n, 1)
                    load_group(0, 2)
                    load_group(0, 3)

                    for n in range(4):
                        store_parts(1, n, 1)

                    def move_max(g):
                        par = g % 2
                        sp.wait_ge(max_split, g + 1)
                        for t in range(PARTS):
                            sp.dma_start(max_scratch[par, t].rearrange("j (r n) -> (j r) n", n=P),
                                         mpart[:, t, :]).then_inc(max_out, 16)
                        sp.wait_ge(max_out, 16 * PARTS * (g + 1))
                        sp.dma_start(turned[STACK:STACK + PARTS, par, 0, :].rearrange("p (h n) -> p h n", h=GROUP),
                                     max_scratch[par]).then_inc(max_in[par], 16)

                    load_group(1, 0)
                    load_group(1, 1)
                    move_max(0)
                    move_max(1)
                    load_group(1, 2)
                    move_max(2)
                    load_group(1, 3)
                    move_max(3)
                    sp.wait_ge(normed, 3)
                    sp.dma_start(rows_b[:, :, 0:D], xn[:]).then_inc(out_done, 16)
                    sp.wait_ge(onehot_ready, 1)
                    sp.dma_start(chosen_b, onehot[:]).then_inc(out_done, 16)
                    for h in range(2):
                        wait_drained(sp, ("b2", h))
                    sp.dma_start(rows_b[:, :, D:2 * D], xs[:]).then_inc(out_done, 16)
                    sp.wait_ge(out_done, 48)

                @block.tensor
                def _(pe):
                    def take(key):
                        n = SLOT[key]
                        if n >= SLOTS:
                            pe.wait_ge(slot_drained[n % SLOTS], n // SLOTS)
                        return slots[n % SLOTS]

                    def give(key, ins):
                        ins.then_inc(slot_filled[SLOT[key] % SLOTS], 1)

                    def transposes(key, src):
                        slot = take(key)
                        for t in range(TT):
                            last = nc.tensor.transpose(slot[:, t * P:(t + 1) * P], src(t), idf[:])
                        give(key, last)

                    def project(a, u):
                        tensor, blk = UNITS[u]
                        key = ("proj", a, u)
                        slot = take(key)
                        for half in range(2):
                            cols = slice(half * HALF, (half + 1) * HALF)
                            if a == 1 and tensor == "k":
                                pairs = [(wuk_sb[:, blk * P:(blk + 1) * P], latt[:, cols])]
                            elif a == 1:
                                pairs = [(wq_sb[:, c, blk * P:(blk + 1) * P], xt[:, c, cols]) for c in range(DC)]
                            else:
                                at = (tensor == "k") * D + blk * P
                                pairs = [(wqkv_sb[:, c, at:at + P], xt[:, c, cols]) for c in range(DC)]
                            for c, (w, r) in enumerate(pairs):
                                last = nc.tensor.matmul(slot[:, cols], w, r, start=c == 0, stop=c == len(pairs) - 1)
                        give(key, last)

                    def swap(a, n):
                        u = ORDER[a][n]
                        key = ("swap", a, u)
                        wait_drained(pe, ("proj", a, u))
                        slot = take(key)
                        for half in range(2):
                            cols = slice(half * HALF, (half + 1) * HALF)
                            last = nc.tensor.matmul(slot[:, cols], perm_sb[:, a, :], qs[n % 2][:, cols],
                                                    start=True, stop=True)
                        give(key, last)

                    def values(a):
                        for h in range(2):
                            key = ("v", a, h)
                            slot = take(key)
                            for i in range(4):
                                t = 4 * h + i
                                if a == 0:
                                    pairs = [(xt[:, c, t * P:(t + 1) * P], wqkv_sb[:, c, 2 * D:3 * D])
                                             for c in range(DC)]
                                else:
                                    pairs = [(latt[:, t * P:(t + 1) * P], wuv_sb[:])]
                                for c, (l, r) in enumerate(pairs):
                                    last = nc.tensor.matmul(slot[:, i * D:(i + 1) * D], l, r,
                                                            start=c == 0, stop=c == len(pairs) - 1)
                            give(key, last)

                    def out_project(a, w):
                        for h in range(2):
                            key = ("op", a, h)
                            slot = take(key)
                            for i in range(4):
                                t = 4 * h + i
                                for c in range(DC):
                                    last = nc.tensor.matmul(slot[:, i * D:(i + 1) * D], xt[:, c, t * P:(t + 1) * P],
                                                            w[:, c, :], start=c == 0, stop=c == DC - 1)
                            give(key, last)

                    def head(buf, par, side, j, rows):
                        return buf[0:rows, par, side, j * T:(j + 1) * T]

                    def attention(a):
                        rows = STACK + PARTS * a
                        for item in SCHED[a]:
                            kind = item[0]
                            if kind == "num":
                                s, pair = item[2:]
                                g, i = divmod(s, NSTEP)
                                half, kb, lo, w = STEPS[i]
                                diagonal = lo == kb * P
                                if i == 0 and pair == 0:
                                    if a == 0:
                                        pe.wait_ge(stack_in[g % 2], 16 * 18 * (g // 2 + 1))
                                    else:
                                        pe.wait_ge(max_in[g % 2], 16 * (g // 2 + 1))
                                slot = take(item)
                                for k in range(2):
                                    j = 2 * pair + k
                                    dst = slot[:, k * HALF:k * HALF + w]
                                    last = nc.tensor.matmul(
                                        dst, head(turned, g % 2, 1, j, rows)[:, kb * P:(kb + 1) * P],
                                        head(turned, g % 2, 0, j, rows)[:, lo:lo + w], start=True, stop=not diagonal)
                                    if diagonal:
                                        last = nc.tensor.matmul(dst[:, 0:P], idb[:], mask_sb[:, 0, :],
                                                                start=False, stop=True)
                                give(item, last)
                            elif kind == "den":
                                g, j, qb = item[2:]
                                slot = take(item)
                                for half in range(2):
                                    cols = slice(half * HALF, (half + 1) * HALF)
                                    last = nc.tensor.matmul(slot[:, cols], head(plain, g % 2, 0, j, rows)[:, qb * P:(qb + 1) * P],
                                                            head(plain, g % 2, 1, j, rows)[:, cols], start=True, stop=True)
                                give(item, last)
                            elif kind == "max":
                                g, j, qb = item[2:]
                                if j == 0 and qb == 0:
                                    pe.wait_ge(stack_in[g % 2], 16 * (36 + 9 * (g // 2 + 1)))
                                slot = take(item)
                                w = (qb + 1) * P
                                lhs = head(turned, g % 2, 0, j, STACK)[:, qb * P:(qb + 1) * P]
                                for at in range(0, w, HALF):
                                    end = min(at + HALF, w)
                                    last = nc.tensor.matmul(slot[:, at:end], lhs, head(turned, g % 2, 1, j, STACK)[:, at:end],
                                                            start=True, stop=end < w)
                                last = nc.tensor.matmul(slot[:, w - P:w], idb[:], mask_sb[:, 1, :], start=False, stop=True)
                                give(item, last)
                            elif kind == "pv":
                                s = item[2]
                                g, i = divmod(s, NSTEP)
                                half, kb, lo, w = STEPS[i]
                                for pair in range(2):
                                    wait_drained(pe, ("num", a, s, pair))
                                n = 8 * a + 2 * g + half
                                if kb == 0 and n >= 1:
                                    pe.wait_ge(o_drained, n)
                                for j in range(GROUP):
                                    last = nc.tensor.matmul(
                                        o_bank[VC * j:VC * (j + 1), lo - half * HALF:HALF],
                                        vs[:, kb, GROUP * g + j, :], prob[:, s % 2, j * HALF:j * HALF + w],
                                        start=kb == 0, stop=closes(s), tile_position=(0, VC * j))
                                last.then_inc(pv_done, 1)
                            elif kind == "ot":
                                g, half = item[2:]
                                n = 8 * a + 2 * g + half
                                pe.wait_ge(o_drained, n + 1)
                                if BANK[item] >= 1:
                                    pe.wait_ge(t_drained, BANK[item])
                                for i in range(4):
                                    last = nc.tensor.transpose(t_bank[:, i * P:(i + 1) * P],
                                                               o_sb[:, n % 2, i * P:(i + 1) * P], idf[:])
                                last.then_inc(t_filled, 1)
                            elif kind == "mx":
                                g = item[2]
                                wait_drained(pe, ("max", a, g, GROUP - 1, TT - 1))
                                if BANK[item] >= 1:
                                    pe.wait_ge(t_drained, BANK[item])
                                nc.tensor.transpose(t_bank[0:GROUP * TT, 0:P], maxes[:, :], idf[:]).then_inc(t_filled, 1)

                    pe.wait_ge(normed, 1)
                    for c in range(DC):
                        transposes(("xt", 0, c), lambda t: xn[:, t, c * P:(c + 1) * P])
                    for c in range(DC):
                        wait_drained(pe, ("xt", 0, c))
                    project(0, 0)
                    project(0, 1)
                    for n in range(NU):
                        swap(0, n)
                        if n + 2 < NU:
                            project(0, n + 2)
                    values(0)
                    for h in range(2):
                        wait_drained(pe, ("v", 0, h))
                    attention(0)
                    pe.wait_ge(t_drained, BANK[("ot", 0, GROUPS - 1, 1)] + 1)
                    for c in range(DC):
                        transposes(("yt", 0, c), lambda t: xn[:, t, c * P:(c + 1) * P])
                    for c in range(DC):
                        wait_drained(pe, ("yt", 0, c))
                    out_project(0, wout_sb)
                    pe.wait_ge(normed, 2)
                    for c in range(DC):
                        transposes(("xt", 1, c), lambda t: xn[:, t, c * P:(c + 1) * P])
                    for c in range(DC):
                        wait_drained(pe, ("xt", 1, c))
                    slot = take(("lat",))
                    for t in range(TT):
                        for c in range(DC):
                            last = nc.tensor.matmul(slot[:, t * P:(t + 1) * P], xt[:, c, t * P:(t + 1) * P],
                                                    wdkv_sb[:, c, :], start=c == 0, stop=c == DC - 1)
                    give(("lat",), last)
                    project(1, 0)
                    project(1, 2)
                    wait_drained(pe, ("lat",))
                    transposes(("lt",), lambda t: latn[:, t * P:(t + 1) * P])
                    swap(1, 0)
                    swap(1, 1)
                    wait_drained(pe, ("lt",))
                    project(1, 1)
                    project(1, 3)
                    swap(1, 2)
                    swap(1, 3)
                    values(1)
                    for h in range(2):
                        wait_drained(pe, ("v", 1, h))
                    attention(1)
                    pe.wait_ge(t_drained, BANK[("ot", 1, GROUPS - 1, 1)] + 1)
                    for c in range(DC):
                        transposes(("yt", 1, c), lambda t: xn[:, t, c * P:(c + 1) * P])
                    for c in range(DC):
                        wait_drained(pe, ("yt", 1, c))
                    out_project(1, wo_sb)
                    pe.wait_ge(normed, 3)
                    for c in range(DC):
                        transposes(("xt", 2, c), lambda t: xn[:, t, c * P:(c + 1) * P])
                    for c in range(DC):
                        wait_drained(pe, ("xt", 2, c))
                    slot = take(("gate",))
                    for t in range(TT):
                        for c in range(DC):
                            last = nc.tensor.matmul(slot[:, t * EXPERTS:(t + 1) * EXPERTS], xt[:, c, t * P:(t + 1) * P],
                                                    gate_sb[:, c, :], start=c == 0, stop=c == DC - 1)
                    give(("gate",), last)
                    pe.wait_ge(onehot_ready, 1)
                    slot = take(("oht",))
                    for t in range(TT):
                        last = nc.tensor.transpose(slot[0:EXPERTS, t * P:(t + 1) * P], onehot[:, t, :], idf[:])
                    give(("oht",), last)
                    wait_drained(pe, ("oht",))
                    for h in range(2):
                        slot = take(("b2", h))
                        for i in range(4):
                            t = 4 * h + i
                            last = nc.tensor.matmul(slot[:, i * D:(i + 1) * D], oht[:, t * P:(t + 1) * P], b2_sb[:],
                                                    start=True, stop=True)
                        give(("b2", h), last)
                @block.scalar
                def _(act):
                    def roots(n):
                        act.wait_ge(var_ready, n)
                        nc.scalar.activation(t8[:, 1, :], t8[:, 0, :], ACT.Sqrt).then_inc(std_ready, 1)

                    def evacuate_q(a, n):
                        u = ORDER[a][n]
                        if n >= 2:
                            filled(act, ("swap", a, ORDER[a][n - 2]))
                            act.wait_ge(cos_done, NU * a + n - 1)
                            if a == 0:
                                act.wait_ge(split_done, jobs_before(0, n - 2, 0) + 1)
                        slot = filled(act, ("proj", a, u))
                        nc.scalar.activation(qs[n % 2], slot[:], ACT.Copy).then_inc(drained(("proj", a, u)), 1)

                    def evacuate_v(a):
                        for h in range(2):
                            slot = filled(act, ("v", a, h))
                            nc.scalar.activation(vs[:, 4 * h:4 * h + 4, :, 0:HD],
                                                 slot[:].rearrange("p (t h d) -> p t h d", t=4, h=HEADS),
                                                 ACT.Copy).then_inc(drained(("v", a, h)), 1)

                    def attention(a):
                        for item in SCHED[a]:
                            if item[0] == "num":
                                s, pair = item[2:]
                                w = STEPS[s % NSTEP][3]
                                if pair == 0 and s >= 2:
                                    act.wait_ge(pv_done, NALL * a + s - 1)
                                slot = filled(act, item)
                                dst = prob[:, s % 2, 2 * pair * HALF:(2 * pair + 2) * HALF]
                                nc.scalar.activation(dst.rearrange("p (h n) -> p h n", h=2)[:, :, 0:w],
                                                     slot[:].rearrange("p (h n) -> p h n", h=2)[:, :, 0:w],
                                                     ACT.Exp, scale=SCALE).then_inc(drained(item), 1)
                            elif item[0] == "den":
                                g, j, qb = item[2:]
                                slot = filled(act, item)
                                h = GROUP * g + j
                                nc.scalar.activation(slot[:], slot[:], ACT.Exp, scale=SCALE,
                                                     accum_out=sums[:, qb, h:h + 1]).then_inc(drained(item), 1)

                    roots(1)
                    slot = filled(act, ("xt", 0, 0))
                    nc.scalar.activation(xt[:, 0, :], slot[:], ACT.Copy).then_inc(drained(("xt", 0, 0)), 1)
                    for n in range(NU):
                        evacuate_q(0, n)
                    evacuate_v(0)
                    attention(0)
                    slot = filled(act, ("yt", 0, 0))
                    nc.scalar.activation(xt[:, 0, :], slot[:], ACT.Copy).then_inc(drained(("yt", 0, 0)), 1)
                    roots(2)
                    roots(3)
                    slot = filled(act, ("xt", 1, 0))
                    nc.scalar.activation(xt[:, 0, :], slot[:], ACT.Copy,
                                         scale=norms_sb[:, 0, 0:1]).then_inc(drained(("xt", 1, 0)), 1)
                    roots(4)
                    for n in range(NU):
                        evacuate_q(1, n)
                    evacuate_v(1)
                    attention(1)
                    slot = filled(act, ("yt", 1, 0))
                    nc.scalar.activation(xt[:, 0, :], slot[:], ACT.Copy).then_inc(drained(("yt", 1, 0)), 1)
                    roots(5)
                    slot = filled(act, ("xt", 2, 0))
                    nc.scalar.activation(xt[:, 0, :], slot[:], ACT.Copy,
                                         scale=norms_sb[:, 1, 0:1]).then_inc(drained(("xt", 2, 0)), 1)
                @block.gpsimd
                def _(pool):
                    pool.wait_ge(normed, 1)
                    nc.gpsimd.tensor_tensor(xs[:], xs[:], bout_sb[:].unsqueeze(1).to_broadcast([P, TT, D]),
                                            ALU.add).then_inc(bias_added, 1)

                    def cosines(a, n):
                        u = ORDER[a][n]
                        wait_drained(pool, ("proj", a, u))
                        if NU * a + n >= 1:
                            pool.wait_ge(rot_done, NU * a + n)
                        nc.gpsimd.tensor_tensor(cosq, qs[n % 2], cos_sb[:, a, :], ALU.mult).then_inc(cos_done, 1)

                    for n in range(NU):
                        cosines(0, n)
                    for n in range(NU):
                        cosines(1, n)

                @block.vector
                def _(dve):
                    steps = [0]

                    def link(ins):
                        steps[0] += 1
                        ins.then_inc(v_step, 1)
                        dve.wait_ge(v_step, steps[0])

                    def token_stats(src):
                        for t in range(TT):
                            ins = nc.vector.bn_stats(stats[:, t, :], src(t))
                        link(ins)
                        for t in range(TT):
                            ins = nc.vector.bn_aggr(mv[:, t, :], stats[:, t, :])
                        link(ins)

                    def inverse_root(n, src, eps, dst):
                        nc.vector.tensor_scalar(t8[:, 0, :], src, eps, None, ALU.add).then_inc(var_ready, 1)
                        dve.wait_ge(std_ready, n)
                        link(nc.vector.reciprocal(dst, t8[:, 1, :]))

                    def split(a, n, rotated, src):
                        job = jobs_before(a, n, rotated)
                        par = job % 2
                        if job >= 2:
                            dve.wait_ge(parts_out[par], 16 * PARTS * (job // 2))
                        link(nc.vector.tensor_copy(parts[:, par, 0, :], src))
                        link(nc.vector.tensor_tensor(rest[:], src, parts[:, par, 0, :], ALU.subtract))
                        link(nc.vector.tensor_copy(parts[:, par, 1, :], rest[:]))
                        nc.vector.tensor_tensor(parts[:, par, 2, :], rest[:], parts[:, par, 1, :],
                                                ALU.subtract).then_inc(split_done, 1)
                        dve.wait_ge(split_done, job + 1)

                    def plain_parts(n):
                        wait_drained(dve, ("proj", 0, ORDER[0][n]))
                        split(0, n, 0, qs[n % 2])

                    def rotate(a, n):
                        key = ("swap", a, ORDER[a][n])
                        slot = filled(dve, key)
                        nc.vector.tensor_tensor(rot, slot[:], sin_sb[:, a, :], ALU.mult).then_inc(drained(key), 1)
                        wait_drained(dve, key)
                        dve.wait_ge(cos_done, NU * a + n + 1)
                        nc.vector.tensor_tensor(rot, rot, cosq, ALU.add).then_inc(rot_done, 1)
                        dve.wait_ge(rot_done, NU * a + n + 1)
                        split(a, n, 1, rot)

                    def attention(a):
                        for item in SCHED[a]:
                            if item[0] == "max":
                                g, j, qb = item[2:]
                                slot = filled(dve, item)
                                if g >= 1 and j == 0 and qb == 0:
                                    dve.wait_ge(t_filled, BANK[("mx", a, g - 1)] + 1)
                                at = j * TT + qb
                                nc.vector.reduce_max(maxes[:, at:at + 1], slot[:, 0:(qb + 1) * P],
                                                     AX_X).then_inc(drained(item), 1)
                            elif item[0] == "mx":
                                g = item[2]
                                dve.wait_ge(t_filled, BANK[item] + 1)
                                if g >= 1:
                                    dve.wait_ge(max_out, 16 * PARTS * g)
                                nc.vector.tensor_scalar(mrow[:, 0, :], t_bank[0:GROUP * TT, 0:P], -1.0, None,
                                                        ALU.mult).then_inc(t_drained, 1)
                                dve.wait_ge(t_drained, BANK[item] + 1)
                                link(nc.vector.tensor_copy(mpart[:, 0, :], mrow[:, 0, :]))
                                link(nc.vector.tensor_tensor(mrow[:, 1, :], mrow[:, 0, :], mpart[:, 0, :], ALU.subtract))
                                link(nc.vector.tensor_copy(mpart[:, 1, :], mrow[:, 1, :]))
                                nc.vector.tensor_tensor(mpart[:, 2, :], mrow[:, 1, :], mpart[:, 1, :],
                                                        ALU.subtract).then_inc(max_split, 1)
                            elif item[0] == "pv" and closes(item[2]):
                                n = HALVES[item]
                                dve.wait_ge(pv_done, NALL * a + item[2] + 1)
                                nc.vector.tensor_copy(o_sb[:, n % 2, :], o_bank[:]).then_inc(o_drained, 1)
                            elif item[0] == "ot":
                                g, half = item[2:]
                                rc = recip[:].rearrange("p (t h) -> p t h", t=4)
                                turned_o = t_bank[:].rearrange("p (t h c) -> p t h c", t=4, h=GROUP)
                                dve.wait_ge(t_filled, BANK[item] + 1)
                                if a == 0:
                                    wait_drained(dve, ("den", 0, g, GROUP - 1, 4 * half + 3))
                                    link(nc.vector.reciprocal(rc, sums[:, 4 * half:4 * half + 4, GROUP * g:GROUP * (g + 1)]))
                                else:
                                    link(nc.vector.reciprocal(rc.unsqueeze(3), turned_o[:, :, :, HD:HD + 1]))
                                dst = xn[:, 4 * half:4 * half + 4, :].rearrange("p t (h d) -> p t h d", h=HEADS)
                                nc.vector.tensor_tensor(dst[:, :, GROUP * g:GROUP * (g + 1), :], turned_o[:, :, :, 0:HD],
                                                        rc.unsqueeze(3).to_broadcast([P, 4, GROUP, HD]),
                                                        ALU.mult).then_inc(t_drained, 1)

                    def residual(dst, key, h):
                        slot = filled(dve, key)
                        part = dst[:, 4 * h:4 * h + 4, :].rearrange("p t d -> p (t d)")
                        nc.vector.tensor_tensor(part, slot[:], part, ALU.add).then_inc(drained(key), 1)
                        wait_drained(dve, key)

                    dve.wait_ge(x_landed, 16)
                    token_stats(lambda t: xs[:, t, :])
                    inverse_root(1, mv[:, :, 1], 1e-5, t8[:, 2, :])
                    for t in range(TT):
                        ins = nc.vector.tensor_scalar(xn[:, t, :], xs[:, t, :], mv[:, t, 0:1], t8[:, 2, t:t + 1],
                                                      ALU.subtract, ALU.mult)
                    ins.then_inc(normed, 1)
                    slot = filled(dve, ("xt", 0, 1))
                    nc.vector.tensor_copy(xt[:, 1, :], slot[:]).then_inc(drained(("xt", 0, 1)), 1)
                    for n in range(NU):
                        plain_parts(n)
                        rotate(0, n)
                    attention(0)
                    slot = filled(dve, ("yt", 0, 1))
                    nc.vector.tensor_copy(xt[:, 1, :], slot[:]).then_inc(drained(("yt", 0, 1)), 1)
                    dve.wait_ge(bias_added, 1)
                    for h in range(2):
                        residual(xs, ("op", 0, h), h)
                    token_stats(lambda t: xs[:, t, :])
                    inverse_root(2, mv[:, :, 1], 1e-5, t8[:, 2, :])
                    link(nc.vector.tensor_tensor(t8[:, 3, :], mv[:, :, 1], t8[:, 2, :], ALU.mult))
                    link(nc.vector.tensor_tensor(t8[:, 3, :], t8[:, 3, :], t8[:, 2, :], ALU.mult))
                    inverse_root(3, t8[:, 3, :], 1e-6, t8[:, 4, :])
                    for t in range(TT):
                        ins = nc.vector.tensor_scalar(zs[:, t, :], xs[:, t, :], mv[:, t, 0:1], t8[:, 2, t:t + 1],
                                                      ALU.subtract, ALU.mult)
                    link(ins)
                    for t in range(TT):
                        ins = nc.vector.tensor_scalar(xn[:, t, :], zs[:, t, :], t8[:, 4, t:t + 1], None, ALU.mult)
                    ins.then_inc(normed, 1)
                    slot = filled(dve, ("xt", 1, 1))
                    nc.vector.tensor_scalar(xt[:, 1, :], slot[:], norms_sb[:, 0, 1:2], None,
                                            ALU.mult).then_inc(drained(("xt", 1, 1)), 1)
                    slot = filled(dve, ("lat",))
                    lat_slot = slot
                    token_stats(lambda t: lat_slot[:, t * P:(t + 1) * P])
                    inverse_root(4, mv[:, :, 1], 1e-5, t8[:, 2, :])
                    for t in range(TT):
                        ins = nc.vector.tensor_scalar(latn[:, t * P:(t + 1) * P], slot[:, t * P:(t + 1) * P],
                                                      mv[:, t, 0:1], t8[:, 2, t:t + 1], ALU.subtract, ALU.mult)
                    ins.then_inc(drained(("lat",)), 1)
                    wait_drained(dve, ("lat",))
                    slot = filled(dve, ("lt",))
                    nc.vector.tensor_scalar(latt, slot[:], ln_sb[:, 0:1], ln_sb[:, 1:2], ALU.mult,
                                            ALU.add).then_inc(drained(("lt",)), 1)
                    for n in range(NU):
                        rotate(1, n)
                    attention(1)
                    slot = filled(dve, ("yt", 1, 1))
                    nc.vector.tensor_copy(xt[:, 1, :], slot[:]).then_inc(drained(("yt", 1, 1)), 1)
                    for h in range(2):
                        residual(zs, ("op", 1, h), h)
                    token_stats(lambda t: zs[:, t, :])
                    link(nc.vector.tensor_tensor(t8[:, 3, :], mv[:, :, 0], mv[:, :, 0], ALU.mult))
                    link(nc.vector.tensor_tensor(t8[:, 3, :], t8[:, 3, :], mv[:, :, 1], ALU.add))
                    inverse_root(5, t8[:, 3, :], 1e-6, t8[:, 4, :])
                    for t in range(TT):
                        ins = nc.vector.tensor_scalar(xn[:, t, :], zs[:, t, :], t8[:, 4, t:t + 1], None, ALU.mult)
                    ins.then_inc(normed, 1)
                    nc.vector.tensor_tensor(xs[:], xs[:], zs[:], ALU.add).then_inc(xr_done, 1)
                    slot = filled(dve, ("xt", 2, 1))
                    nc.vector.tensor_scalar(xt[:, 1, :], slot[:], norms_sb[:, 1, 1:2], None,
                                            ALU.mult).then_inc(drained(("xt", 2, 1)), 1)
                    slot = filled(dve, ("gate",))
                    nc.vector.tensor_tensor(logits[:], slot[:, 0:TT * EXPERTS].rearrange("p (t e) -> p t e", e=EXPERTS),
                                            gate_b_sb[:].unsqueeze(1).to_broadcast([P, TT, EXPERTS]),
                                            ALU.add).then_inc(drained(("gate",)), 1)
                    wait_drained(dve, ("gate",))
                    link(nc.vector.reduce_max(top[:], logits[:], AX_X))
                    link(nc.vector.tensor_tensor(onehot[:], logits[:], top[:].unsqueeze(2).to_broadcast([P, TT, EXPERTS]),
                                                 ALU.is_ge))
                    link(nc.vector.tensor_copy(top[:], onehot[:, :, 0]))
                    for e in range(1, EXPERTS):
                        ins = nc.vector.tensor_tensor(onehot[:, :, e], onehot[:, :, e], top[:], ALU.is_gt)
                        if e < EXPERTS - 1:
                            link(ins)
                            link(nc.vector.tensor_tensor(top[:], top[:], onehot[:, :, e], ALU.max))
                    ins.then_inc(onehot_ready, 1)
                    dve.wait_ge(onehot_ready, 1)
                    slot = filled(dve, ("oht",))
                    nc.vector.tensor_copy(oht[:], slot[0:EXPERTS, :]).then_inc(drained(("oht",)), 1)
                    dve.wait_ge(xr_done, 1)
                    for h in range(2):
                        residual(xs, ("b2", h), h)

            for s in in_loop:
                nc.sync.sem_clear(s)
            nc.all_engine_barrier()


def build_experts(nc, rows, chosen, norms, w1, b1, w2, ident_f, before, starts, tile_ids, token_ids, no_token,
                  zero_row, out):
    table = nc.dram_tensor("token_of_slot", (P * TILES, 1), U32, kind="Internal").ap()
    out_rows = out.rearrange("b t d -> (b t) d")
    NT = B * TT
    with ExitStack() as ctx:
        def sb(name, shape, dt=F32):
            return ctx.enter_context(nc.sbuf_tensor(name, shape, dt))

        def sem(name):
            return ctx.enter_context(nc.semaphore(name))

        def pb(name, shape):
            return ctx.enter_context(nc.psum_tensor(name, shape, F32))

        h_ps = pb("h_ps", [P, HID])
        ht_ps = pb("ht_ps", [P, HC, P])
        y_ps = [pb(f"y_ps{i}", [P, HALF]) for i in range(2)]
        x_ps = [pb(f"x_ps{i}", [P, HALF]) for i in range(2)]

        w1_sb = sb("w1_sb", [P, EXPERTS, DC * HID])
        w2_sb = sb("w2_sb", [P, EXPERTS, HC * D])
        b1_sb = sb("b1_sb", [P, EXPERTS, HID])
        norms_sb = sb("norms2_sb", [P, 2, DC])
        idf = sb("idf2", [P, P])
        before_sb = sb("before_sb", [P, 2, P])
        starts_sb = sb("starts_sb", [P, NT])
        tile_ids_sb = sb("tile_ids_sb", [P, TILES])
        token_ids_sb = sb("token_ids_sb", [P, NT], U32)
        oh = sb("oh", [P, NT, EXPERTS])
        upto = [sb(f"upto{i}", [P, NT, EXPERTS]) for i in range(2)]
        slot_of = sb("slot_of", [P, NT, EXPERTS])
        passed = sb("passed", [P, EXPERTS, NT])
        tiles = sb("tiles", [P, EXPERTS])
        ends = sb("ends", [P, EXPERTS])
        first = sb("first", [P, EXPERTS])
        slot_f = sb("slot_f", [P, NT])
        slot_i = sb("slot_i", [P, NT], I32)
        slot_lo = sb("slot_lo", [P, NT], I32)
        slot_hi = sb("slot_hi", [P, NT], I32)
        place = sb("place", [P, NT], U32)
        tile_expert_f = sb("tile_expert_f", [P, TILES])
        tile_expert = sb("tile_expert", [P, TILES], I32)
        tokens = sb("tokens", [P, TILES], U32)
        now = sb("now", [P, UNROLL], U32)
        xg = sb("xg", [P, GATHERED, 2 * D])
        xgt = sb("xgt", [P, 2, DC * P])
        hs = sb("hs", [P, 2, HID])
        hst = sb("hst", [P, 2, HC, P])
        yo = sb("yo", [P, GATHERED, D])

        s_const = sem("s_const2")
        w_landed = sem("w_landed")
        table_cleared = sem("table_cleared")
        ranked = sem("ranked")
        d_step = sem("d_step")
        placed = sem("placed")
        scattered = sem("scattered")
        tokens_in = sem("tokens_in")
        experts_ready = sem("experts_ready")
        now_ready = sem("now_ready")
        gathered = [sem(f"gathered{i}") for i in range(GATHERED)]
        stored = [sem(f"stored{i}") for i in range(GATHERED)]
        x_turned = sem("x_turned")
        x_drained = sem("x_drained")
        h_made = sem("h_made")
        h_drained = sem("h_drained")
        h_turned = sem("h_turned")
        ht_drained = sem("ht_drained")
        y_made = sem("y_made")
        y_added = sem("y_added")

        consts = [(norms_sb, norms), (idf, ident_f), (before_sb, before), (starts_sb, starts),
                  (tile_ids_sb, tile_ids), (token_ids_sb, token_ids)]
        with nc.Block() as block:
            @block.sync
            def _(sp):
                for dst, src in consts:
                    sp.dma_start(dst[:], src).then_inc(s_const, 16)
                sp.dma_start(oh[:].rearrange("p (b t) e -> p b t e", b=B),
                             chosen.rearrange("b p t e -> p b t e")).then_inc(s_const, 16)
                sp.dma_start(table.rearrange("(p t) o -> p (t o)", p=P), no_token).then_inc(table_cleared, 16)
                sp.dma_start(rows[B * T:B * T + 1], zero_row).then_inc(table_cleared, 16)
                for e in range(EXPERTS):
                    sp.dma_start(w1_sb[:, e], w1[e]).then_inc(w_landed, 16)
                    sp.dma_start(w2_sb[:, e], w2[e]).then_inc(w_landed, 16)
                sp.dma_start(b1_sb[:], b1).then_inc(w_landed, 16)
                sp.wait_ge(scattered, 16 * NT)
                sp.dma_start(tokens[:], table.rearrange("(p t) o -> p (t o)", p=P)).then_inc(tokens_in, 16)
                sp.wait_ge(tokens_in, 16)

            @block.tensor
            def _(pe):
                pe.wait_ge(s_const, 16 * (len(consts) + 1))
                oh_flat = oh[:].rearrange("p t e -> p (t e)")
                nc.tensor.matmul(h_ps[:, 0:NT * EXPERTS], before_sb[:, 0, :], oh_flat, start=True, stop=True)
                nc.tensor.matmul(h_ps[:, HALF:HALF + NT * EXPERTS], before_sb[:, 1, :], oh_flat,
                                 start=True, stop=True).then_inc(ranked, 1)

            @block.vector
            def _(dve):
                steps = [0]

                def link(ins):
                    steps[0] += 1
                    ins.then_inc(d_step, 1)
                    dve.wait_ge(d_step, steps[0])

                dve.wait_ge(ranked, 1)
                rank = h_ps[:, 0:NT * EXPERTS].rearrange("p (t e) -> p t e", e=EXPERTS)
                total = h_ps[:, HALF:HALF + NT * EXPERTS].rearrange("p (t e) -> p t e", e=EXPERTS)
                a, z = upto
                link(nc.vector.tensor_copy(a[:], total))
                n = 1
                while n < NT:
                    nc.vector.tensor_copy(z[:, 0:n, :], a[:, 0:n, :])
                    link(nc.vector.tensor_tensor(z[:, n:, :], a[:, n:, :], a[:, 0:NT - n, :], ALU.add))
                    a, z = z, a
                    n *= 2
                link(nc.vector.tensor_tensor(passed[:], starts_sb[:].unsqueeze(1).to_broadcast([P, EXPERTS, NT]),
                                             a[:, NT - 1, :].unsqueeze(2).to_broadcast([P, EXPERTS, NT]), ALU.is_lt))
                link(nc.vector.reduce_sum(tiles[:], passed[:], AX_X))
                link(nc.vector.tensor_copy(ends[:], tiles[:]))
                for e in range(1, EXPERTS):
                    link(nc.vector.tensor_tensor(ends[:, e:e + 1], ends[:, e - 1:e], tiles[:, e:e + 1], ALU.add))
                link(nc.vector.tensor_tensor(first[:], ends[:], tiles[:], ALU.subtract))
                link(nc.vector.tensor_scalar(first[:], first[:], float(P), None, ALU.mult))
                link(nc.vector.tensor_tensor(slot_of[:], total, a[:], ALU.subtract))
                link(nc.vector.tensor_tensor(slot_of[:], rank, slot_of[:], ALU.subtract))
                link(nc.vector.tensor_tensor(slot_of[:], slot_of[:], first[:].unsqueeze(1).to_broadcast([P, NT, EXPERTS]),
                                             ALU.add))
                link(nc.vector.tensor_tensor(slot_of[:], slot_of[:], oh[:], ALU.mult))
                link(nc.vector.reduce_sum(slot_f[:], slot_of[:], AX_X))
                link(nc.vector.tensor_copy(slot_i[:], slot_f[:]))
                link(nc.vector.tensor_scalar(slot_lo[:], slot_i[:], P - 1, None, ALU.bitwise_and))
                link(nc.vector.tensor_scalar(slot_hi[:], slot_i[:], P.bit_length() - 1, None, ALU.logical_shift_right))
                nc.vector.scalar_tensor_tensor(out=place[:], in0=slot_lo[:], scalar=float(TILES), in1=slot_hi[:],
                                               op0=ALU.mult, op1=ALU.add).then_inc(placed, 1)
                link(nc.vector.tensor_scalar(tile_expert_f[:], tile_ids_sb[:], ends[:, 0:1], None, ALU.is_ge))
                for e in range(1, EXPERTS - 1):
                    link(nc.vector.scalar_tensor_tensor(out=tile_expert_f[:], in0=tile_ids_sb[:], scalar=ends[:, e:e + 1],
                                                        in1=tile_expert_f[:], op0=ALU.is_ge, op1=ALU.add))
                nc.vector.tensor_copy(tile_expert[:], tile_expert_f[:]).then_inc(experts_ready, 1)
                dve.wait_ge(experts_ready, 1)

            @block.gpsimd
            def _(pool):
                pool.wait_ge(placed, 1)
                pool.wait_ge(table_cleared, 32)
                for t in range(NT):
                    pool.indirect_dma_start(table, bass.IndirectOffsetOnAxis(ap=place[:, t:t + 1], axis=0),
                                            token_ids_sb[:, t:t + 1], None).then_inc(scattered, 16)

        in_loop = ([now_ready, x_turned, x_drained, h_made, h_drained, h_turned, ht_drained, y_made, y_added])

        def over_rounds(r, i, n):
            return r * (16 * len(range(i, UNROLL, GATHERED))) + 16 * n

        with nc.Fori(0, TILES // UNROLL, 1) as r:
            with nc.Block() as block:
                @block.gpsimd
                def _(pool):
                    def gather(k):
                        if k >= GATHERED:
                            pool.wait_ge(y_added, k - GATHERED + 1)
                        pool.indirect_dma_start(
                            xg[:, k % GATHERED, :], None, rows,
                            bass.IndirectOffsetOnAxis(ap=now[:, k:k + 1], axis=0)).then_inc(gathered[k % GATHERED], 16)

                    def store(k):
                        pool.wait_ge(y_added, k + 1)
                        pool.indirect_dma_start(
                            out_rows, bass.IndirectOffsetOnAxis(ap=now[:, k:k + 1], axis=0),
                            yo[:, k % GATHERED, :], None, bounds_check=B * T - 1,
                            oob_is_err=False).then_inc(stored[k % GATHERED], 16)

                    nc.gpsimd.tensor_copy(now[:], tokens[:, bass.ds(r * UNROLL, UNROLL)]).then_inc(now_ready, 1)
                    pool.wait_ge(now_ready, 1)
                    for k in range(GATHERED):
                        gather(k)
                    for k in range(UNROLL):
                        store(k)
                        if k + GATHERED < UNROLL:
                            gather(k + GATHERED)
                    for i in range(GATHERED):
                        pool.wait_ge(stored[i], over_rounds(r, i, len(range(i, UNROLL, GATHERED))))

                @block.tensor
                def _(pe):
                    def turn_x(k):
                        pe.wait_ge(gathered[k % GATHERED], over_rounds(r, k % GATHERED, k // GATHERED + 1))
                        if k >= 2:
                            pe.wait_ge(x_drained, k - 1)
                        for c in range(DC):
                            last = nc.tensor.transpose(x_ps[k % 2][:, c * P:(c + 1) * P],
                                                       xg[:, k % GATHERED, c * P:(c + 1) * P], idf[:])
                        last.then_inc(x_turned, 1)

                    def hidden(k, e):
                        pe.wait_ge(x_drained, k + 1)
                        if k >= 1:
                            pe.wait_ge(h_drained, k)
                        for half in range(2):
                            for c in range(DC):
                                w = w1_sb[:, bass.ds(e, 1), c * HID + half * HALF:c * HID + (half + 1) * HALF]
                                last = nc.tensor.matmul(h_ps[:, half * HALF:(half + 1) * HALF],
                                                        xgt[:, k % 2, c * P:(c + 1) * P],
                                                        w.rearrange("p e n -> p (e n)"), start=c == 0, stop=c == DC - 1)
                        last.then_inc(h_made, 1)

                    def turn_h(k):
                        pe.wait_ge(h_drained, k + 1)
                        if k >= 1:
                            pe.wait_ge(ht_drained, k)
                        for c in range(HC):
                            last = nc.tensor.transpose(ht_ps[:, c, :], hs[:, k % 2, c * P:(c + 1) * P], idf[:])
                        last.then_inc(h_turned, 1)

                    def outputs(k, e):
                        pe.wait_ge(ht_drained, k + 1)
                        if k >= 2:
                            pe.wait_ge(y_added, k - 1)
                        for c in range(HC):
                            w = w2_sb[:, bass.ds(e, 1), c * D:(c + 1) * D]
                            last = nc.tensor.matmul(y_ps[k % 2][:, 0:D], hst[:, k % 2, c, :],
                                                    w.rearrange("p e n -> p (e n)"), start=c == 0, stop=c == HC - 1)
                        last.then_inc(y_made, 1)

                    experts = {}
                    turn_x(0)
                    pe.wait_ge(w_landed, 16 * (2 * EXPERTS + 1))
                    for k in range(UNROLL + 1):
                        if k < UNROLL:
                            experts[k] = pe.value_load(tile_expert[0:1, bass.ds(r * UNROLL + k, 1)], min_val=0,
                                                       max_val=EXPERTS - 1)
                            if k + 1 < UNROLL:
                                turn_x(k + 1)
                            hidden(k, experts[k])
                        if k >= 1:
                            outputs(k - 1, experts[k - 1])
                        if k < UNROLL:
                            turn_h(k)

                @block.scalar
                def _(act):
                    def move_x(k):
                        act.wait_ge(x_turned, k + 1)
                        if k >= 2:
                            act.wait_ge(h_made, k - 1)
                        for c in range(DC):
                            ins = nc.scalar.activation(xgt[:, k % 2, c * P:(c + 1) * P], x_ps[k % 2][:, c * P:(c + 1) * P],
                                                       ACT.Copy, scale=norms_sb[:, 1, c:c + 1])
                        ins.then_inc(x_drained, 1)

                    move_x(0)
                    for k in range(UNROLL):
                        if k + 1 < UNROLL:
                            move_x(k + 1)
                        act.wait_ge(h_turned, k + 1)
                        if k >= 2:
                            act.wait_ge(y_made, k - 1)
                        nc.scalar.activation(hst[:, k % 2], ht_ps[:], ACT.Relu).then_inc(ht_drained, 1)

                @block.vector
                def _(dve):
                    dve.wait_ge(w_landed, 16 * (2 * EXPERTS + 1))
                    for k in range(UNROLL + 1):
                        if k < UNROLL:
                            e = dve.value_load(tile_expert[0:1, bass.ds(r * UNROLL + k, 1)], min_val=0,
                                               max_val=EXPERTS - 1)
                            dve.wait_ge(h_made, k + 1)
                            if k >= 2:
                                dve.wait_ge(h_turned, k - 1)
                            nc.vector.tensor_tensor(hs[:, k % 2, :], h_ps[:],
                                                    b1_sb[:, bass.ds(e, 1), :].rearrange("p e n -> p (e n)"),
                                                    ALU.add).then_inc(h_drained, 1)
                        if k >= 1:
                            j = k - 1
                            dve.wait_ge(y_made, j + 1)
                            if j >= GATHERED:
                                dve.wait_ge(stored[j % GATHERED], over_rounds(r, j % GATHERED, j // GATHERED))
                            nc.vector.tensor_tensor(yo[:, j % GATHERED, :], y_ps[j % 2][:, 0:D],
                                                    xg[:, j % GATHERED, D:2 * D], ALU.add).then_inc(y_added, 1)

            for s in in_loop:
                nc.sync.sem_clear(s)
            nc.all_engine_barrier()


def kernel(L0_attn_x, L0_attn_w_qkv, L0_attn_w_out, L0_attn_b_out, L0_ffn_norm1_w, L0_ffn_norm2_w, L0_ffn_Wq,
           L0_ffn_Wdkv, L0_ffn_Wuk, L0_ffn_Wuv, L0_ffn_Wo, L0_ffn_ln_g, L0_ffn_ln_b, L0_ffn_gate_w, L0_ffn_gate_b,
           L0_ffn_W1, L0_ffn_b1, L0_ffn_W2, L0_ffn_b2):
    import ml_dtypes
    import numpy as np
    import concourse.bacc as bacc
    from concourse.bass_utils import run_bass_kernel_spmd

    def chunked(w):
        w = np.asarray(w)
        return np.ascontiguousarray(w.T.reshape(-1, P, w.shape[0]).transpose(1, 0, 2))

    def columns(v):
        v = np.asarray(v)
        v = v.reshape(*v.shape[:-1], -1, P)
        return np.ascontiguousarray(np.moveaxis(v, -1, 0))

    def every_partition(v):
        return np.ascontiguousarray(np.broadcast_to(np.asarray(v), (P, np.asarray(v).shape[-1])))

    f32 = np.float32
    half = HD // 2
    pos = np.arange(T, dtype=f32)
    i = np.arange(half, dtype=f32)
    theta0 = (10000.0 ** ((-2.0 * (i - 1.0) / HD).astype(np.float64))).astype(f32)
    theta1 = (1.0 / (10000.0 ** (np.arange(half) / half)).astype(f32)).astype(f32)
    row = np.arange(P)
    d = row % HD
    angle0 = (pos[None, :] * theta0[d // 2][:, None]).astype(np.float64)
    angle1 = (pos[None, :] * theta1[d % half][:, None]).astype(np.float64)
    sign0 = np.where(d % 2 == 0, 1.0, -1.0)[:, None]
    sign1 = np.where(d < half, -1.0, 1.0)[:, None]
    cos = np.stack([np.cos(angle0), np.cos(angle1)], 1).astype(f32)
    sin = np.stack([np.sin(angle0) * sign0, np.sin(angle1) * sign1], 1).astype(f32)
    perm = np.zeros((P, 2, P), f32)
    perm[row ^ 1, 0, row] = 1
    perm[row ^ half, 1, row] = 1
    ident = np.eye(P, dtype=f32)
    at = np.arange(P)
    keys_first = np.where(at[:, None] > at[None, :], MASKED, 0.0)
    mask = np.stack([keys_first, keys_first.T], 1)

    before = np.stack([at[:, None] < at[None, :], np.ones((P, P), bool)], 1).astype(f32)
    NT = B * TT
    token_ids = (at[:, None] + P * np.arange(NT)[None, :]).astype(np.uint32)

    W1, W2 = np.asarray(L0_ffn_W1), np.asarray(L0_ffn_W2)
    arrays = {
        "x": np.asarray(L0_attn_x),
        "wqkv": chunked(L0_attn_w_qkv), "wout": chunked(L0_attn_w_out), "bout": every_partition(L0_attn_b_out),
        "norms": columns(np.stack([np.asarray(L0_ffn_norm1_w), np.asarray(L0_ffn_norm2_w)])),
        "wq": chunked(L0_ffn_Wq), "wdkv": chunked(L0_ffn_Wdkv), "wuk": chunked(L0_ffn_Wuk)[:, 0],
        "wuv": chunked(L0_ffn_Wuv)[:, 0], "wo": chunked(L0_ffn_Wo),
        "lnp": np.ascontiguousarray(np.stack([np.asarray(L0_ffn_ln_g), np.asarray(L0_ffn_ln_b)], 1)),
        "gate": chunked(L0_ffn_gate_w), "gate_b": every_partition(L0_ffn_gate_b),
        "w1": np.stack([chunked(W1[e]).reshape(P, -1) for e in range(EXPERTS)]),
        "b1": np.broadcast_to(np.asarray(L0_ffn_b1), (P, EXPERTS, HID)),
        "w2": np.stack([chunked(W2[e]).reshape(P, -1) for e in range(EXPERTS)]),
        "b2": np.asarray(L0_ffn_b2),
        "before": before, "starts": every_partition(np.arange(NT, dtype=f32) * P),
        "tile_ids": every_partition(np.arange(TILES, dtype=f32)), "token_ids": token_ids,
        "no_token": np.full((P, TILES), B * T, np.uint32), "zero_row": np.zeros((1, 2 * D), f32),
        "cos": cos, "sin": sin, "perm": perm,
        "ident_f": ident, "ident_b": ident.astype(ml_dtypes.bfloat16), "mask_b": mask.astype(ml_dtypes.bfloat16),
    }
    nc = bacc.Bacc("TRN2", target_bir_lowering=False, num_devices=1)
    args = {}
    for name, a in arrays.items():
        arrays[name] = a = np.ascontiguousarray(a)
        args[name] = nc.dram_tensor("in_" + name, a.shape, mybir.dt.from_np(a.dtype), kind="ExternalInput").ap()
    out = nc.dram_tensor("out_x", (B, T, D), F32, kind="ExternalOutput").ap()
    build(nc, **args, out=out)
    r = run_bass_kernel_spmd(nc, [{"in_" + n: a for n, a in arrays.items()}], core_ids=[0])
    return r.results[0]["out_x"]
```

```python
from contextlib import ExitStack

import concourse.bass as bass
from concourse import mybir

P = 128
D = 256
HEADS, HD = 16, 16
LAT = 128
EXPERTS, HID = 4, 1024
B, T = 8, 1024
TT = T // P
DC = D // P
HC = HID // P
HALF = 512
GROUP = 4
GROUPS = HEADS // GROUP
PARTS = 3
TERMS = [(0, 0), (1, 0), (2, 0), (0, 1), (1, 1), (0, 2)]
STACK = len(TERMS) * HD
SCALE = 1.0 / 4.0
MASKED = -1e30
SLOTS = 3

UNROLL = 17
TILES = -(-(B * TT + EXPERTS - 1) // UNROLL) * UNROLL
GATHERED = 4

F32 = mybir.dt.float32
I32 = mybir.dt.int32
U32 = mybir.dt.uint32
BF16 = mybir.dt.bfloat16
ALU = mybir.AluOpType
ACT = mybir.ActivationFunctionType
AX_X = mybir.AxisListType.X

ROOT_GUESS = 0x5F3759DF

STEPS = []
for _h in range(2):
    for _kb in range(4 * _h + 4):
        _lo = max(_kb * P, _h * HALF)
        STEPS.append((_h, _kb, _lo, (_h + 1) * HALF - _lo))
NSTEP = len(STEPS)
NALL = GROUPS * NSTEP
SCORE_SLOTS = [1 if w <= HALF // 2 else 2 for _, _, _, w in STEPS]
UNITS = [("q", 0), ("k", 0), ("q", 1), ("k", 1)]


def closes(s):
    i = s % NSTEP
    return i == NSTEP - 1 or STEPS[i + 1][0] != STEPS[i][0]



def project_first(q):
    items = [(0, ("getx", q)), (0, ("table", 0, q)), (9, ("stat", 0, 0, q)), (10, ("stat", 0, 1, q)), (10, ("root", 0, q)),
             (11, ("norm", 0, 0, q)), (12, ("norm", 0, 1, q)), (13, ("turn", "xt0", 0, q)),
             (14, ("turn", "xt0", 1, q))]
    for u in range(len(UNITS)):
        at = (20, 23, 33, 39)[u]
        items += [(at, ("proj", 0, u, q)), (at + 1, ("split", 0, u, 0, 0, q)), (at + 1, ("swap", 0, u, q)),
                  (at + 1, ("sine", 0, u, q)), (at + 2, ("split", 0, u, 0, 1, q)), (at + 2, ("cosine", 0, u, q)),
                  (at + 2, ("split", 0, u, 1, 0, q)), (at + 3, ("parts", 0, u, 0, q)), (at + 3, ("split", 0, u, 1, 1, q)),
                  (at + 4, ("parts", 0, u, 1, q))]
    items += [(36, ("v", 0, 0, q)), (38, ("v", 0, 1, q))]
    return sorted(items, key=lambda x: x[0])


def project_second(q):
    items = [(0, ("turn", "yt0", 0, q)), (1, ("turn", "yt0", 1, q)), (1, ("table", 1, q)),
             (13, ("residual", q)), (16, ("op", 0, 0, q)), (18, ("op", 0, 1, q)),
             (19, ("stat", 1, 0, q)), (20, ("stat", 1, 1, q)), (20, ("root", 1, q)),
             (21, ("root", 4, q)), (21, ("norm", 1, 0, q)), (22, ("norm", 1, 1, q)),
             (23, ("turn", "xt1", 0, q)), (24, ("turn", "xt1", 1, q)), (25, ("lat", q)), (26, ("stat", 3, 0, q)),
             (26, ("stat", 3, 1, q)), (27, ("root", 3, q)), (28, ("norm", 3, 1, q)),
             (29, ("turn", "lt", 0, q)), (44, ("v", 1, 0, q)), (46, ("v", 1, 1, q))]
    for at, u in ((26, 0), (30, 1), (33, 2), (36, 3)):
        items += [(at, ("proj", 1, u, q)), (at + 1, ("swap", 1, u, q)), (at + 1, ("sine", 1, u, q)),
                  (at + 2, ("cosine", 1, u, q)), (at + 2, ("split", 1, u, 1, 0, q)), (at + 3, ("split", 1, u, 1, 1, q)),
                  (at + 4, ("parts", 1, u, 1, q))]
    return sorted(items, key=lambda x: x[0])


def finish(q):
    return [(2, ("turn", "yt1", 0, q)), (3, ("turn", "yt1", 1, q)), (3, ("op", 1, 0, q)), (5, ("op", 1, 1, q)),
            (5, ("stat", 2, 0, q)), (6, ("stat", 2, 1, q)), (6, ("root", 2, q)),
            (7, ("norm", 2, 0, q)), (7, ("norm", 2, 1, q)), (8, ("sum", q)), (8, ("turn", "xt2", 0, q)),
            (9, ("turn", "xt2", 1, q)), (10, ("gate", q)), (11, ("pick", q)), (12, ("rows", q))]


def spread(own, others):
    items, done = [], 0
    for n, item in enumerate(own):
        upto = (n + 1) * len(others) // len(own)
        items += [item] + others[done:upto]
        done = upto
    return items


def attention(a, q, beside):
    items = []
    beside = list(beside)
    for s in range(NALL):
        g, i = divmod(s, NSTEP)
        half = STEPS[i][0]
        own = [("num", a, s, k, q) for k in range(SCORE_SLOTS[i])]
        late = own[1:] if a == 0 and i < NSTEP - 1 else []
        own = own[:len(own) - len(late)]
        if a == 0:
            per = 16 // (4 * half + 4)
            at = per * (i - 4 * half)
            dens = [("den", a, g, n % GROUP, 4 * half + n // GROUP, q) for n in range(at, at + per)]
            early = per if i == NSTEP - 1 else per // 2
            own += dens[:early]
        if s >= 1:
            own.append(("pv", a, s - 1, q))
        if s >= 2 and closes(s - 2):
            own.append(("ot", a, (s - 2) // NSTEP, STEPS[(s - 2) % NSTEP][0], q))
        own += late
        if a == 0:
            own += dens[early:]
        now = []
        while beside and beside[0][0] <= s:
            now.append(beside.pop(0)[1])
        items += spread(own, now)
    items += [("pv", a, NALL - 1, q), ("ot", a, GROUPS - 1, 1, q)]
    return items + [x for _, x in beside]


def maxima(g, q, at):
    blocks = ([(j, qb) for j in range(0, GROUP, 2) for qb in range(TT // 2)]
              + [(j, qb) for j in range(GROUP) for qb in range(TT // 2, TT)])
    return ([(at + n // 4, ("max", 1, g, j, qb, q)) for n, (j, qb) in enumerate(blocks)]
            + [(at + 5, ("mx", 1, g, q)), (at + 5, ("maxrow", g, q))])


def merged(*lists):
    return sorted((x for items in lists for x in items), key=lambda x: x[0])


def second_attention(q, others):
    beside = [(0, ("group", 1, 1, q)), (NSTEP, ("group", 1, 2, q)), (2 * NSTEP, ("group", 1, 3, q))]
    for g in range(1, GROUPS):
        beside += maxima(g, q, NSTEP * (g - 1) + 2)
    return attention(1, q, merged(beside, others))


def parted(items):
    later = [x for x in items if x[1][0] in ("proj", "swap", "sine", "cosine", "split", "parts")
             and UNITS[x[1][2]][1] == 1]
    before = [x for x in items if x not in later]
    return before, [(max(0, at - later[0][0]), item) for at, item in later]


def items_of_start():
    alone = lambda part: [x for _, x in part]
    values = [(0, ("v", 0, 0, 1)), (0, ("v", 0, 1, 1))]
    groups = [(0, ("group", 0, 1, 0)), (NSTEP, ("group", 0, 2, 0)), (2 * NSTEP, ("group", 0, 3, 0))]
    before, later = parted(project_first(0))
    return (alone(before) + [("group", 0, 0, 0)]
            + attention(0, 0, merged(groups, later, [x for x in project_first(1) if x[1][0] not in ("v", "table")]))
            + alone(values) + [("group", 0, 0, 1)])


def items_of_loop():
    groups = [(0, ("group", 0, 1, 1)), (NSTEP, ("group", 0, 2, 1)), (2 * NSTEP, ("group", 0, 3, 1)),
              (3 * NSTEP, ("group", 1, 0, 0))]
    return (attention(0, 1, merged(finish(-1), project_second(0), groups, maxima(0, 0, 3 * NSTEP + 3)))
            + second_attention(0, merged(project_first(2), [(3 * NSTEP, ("group", 0, 0, 2))])))


def items_of_end():
    alone = lambda part: [x for _, x in part]
    before, later = parted(project_second(0))
    return (alone(merged(finish(-1), before)) + [("group", 1, 0, 0)] + alone(merged(later, maxima(0, 0, 2)))
            + second_attention(0, []) + alone(finish(0)))


class Plan:

    USE_SLOT = ("turn", "proj", "swap", "v", "num", "den", "max", "op", "lat", "gate")

    def __init__(self, items):
        self.items = items

        def number(test):
            return {x: n for n, x in enumerate(x for x in items if test(x))}

        self.slot = number(lambda x: x[0] in self.USE_SLOT)
        self.bank = number(lambda x: x[0] in ("ot", "mx"))
        self.pv = number(lambda x: x[0] == "pv")
        self.half = number(lambda x: x[0] == "pv" and closes(x[2]))
        self.unit = number(lambda x: x[0] == "proj")
        self.swap = number(lambda x: x[0] == "swap")
        self.cosine = number(lambda x: x[0] == "cosine")
        self.job = number(lambda x: x[0] == "split" and x[4] == 1)
        self.root = number(lambda x: x[0] == "root")
        self.normed = number(lambda x: x[0] == "norm" and x[2] == 1)
        self.pick = number(lambda x: x[0] == "pick")
        self.mx = number(lambda x: x[0] == "mx")
        self.getx = number(lambda x: x[0] == "getx")
        self.residual = number(lambda x: x[0] == "residual")
        self.table = number(lambda x: x[0] == "table")
        self.rows = number(lambda x: x[0] == "rows")
        self.at = {x: n for n, x in enumerate(items)}
        self.stacked, self.maxed, count, mcount = {}, {}, [0, 0], [0, 0]
        for x in items:
            if x[0] == "group":
                count[x[2] % 2] += 18 if x[1] == 0 else 9
                self.stacked[x[1:]] = count[x[2] % 2]
            if x[0] == "maxrow":
                mcount[x[1] % 2] += 1
                self.maxed[x[1:]] = mcount[x[1] % 2]
        self.stack_total, self.max_total = count, mcount

    def job_of(self, a, u, rotated, q):
        return self.job.get(("split", a, u, rotated, 1, q))

    def last_before(self, kind_test, item):
        n = self.at[item]
        found = [x for x in self.items[:n] if kind_test(x)]
        return found[-1] if found else None


def build(nc, x, wqkv, wout, bout, norms, wq, wdkv, wuk, wuv, wo, lnp, gate, gate_b, w1, b1, w2, b2,
          cos, sin, perm, ident_f, ident_b, mask_b, before, starts, tile_ids, token_ids, no_token, zero_row, out):
    rows = nc.dram_tensor("rows", ((B + 1) * T + 1, 2 * D), F32, kind="Internal").ap()
    chosen = nc.dram_tensor("chosen", (B + 1, P, TT, EXPERTS), F32, kind="Internal").ap()
    build_sequences(nc, x, wqkv, wout, bout, norms, wq, wdkv, wuk, wuv, wo, lnp, gate, gate_b,
                    cos, sin, perm, ident_f, ident_b, mask_b, rows, chosen)
    build_experts(nc, rows, chosen, norms, w1, b1, w2, b2, ident_f, before, starts, tile_ids, token_ids, no_token,
                  zero_row, out)


def build_sequences(nc, x, wqkv, wout, bout, norms, wq, wdkv, wuk, wuv, wo, lnp, gate, gate_b,
                    cos, sin, perm, ident_f, ident_b, mask_b, rows, chosen):
    scratch = nc.dram_tensor("head_parts", (6, HEADS, PARTS, HD, T), BF16, kind="Internal").ap()
    max_scratch = nc.dram_tensor("max_parts", (2, PARTS, GROUP, T), BF16, kind="Internal").ap()

    with ExitStack() as ctx:
        def sb(name, shape, dt=F32):
            return ctx.enter_context(nc.sbuf_tensor(name, shape, dt))

        def sem(name):
            return ctx.enter_context(nc.semaphore(name))

        slots = [ctx.enter_context(nc.psum_tensor(f"slot{i}", [P, 2 * HALF], F32)) for i in range(SLOTS)]
        o_bank = ctx.enter_context(nc.psum_tensor("o_bank", [P, HALF], F32))
        t_bank = ctx.enter_context(nc.psum_tensor("t_bank", [P, HALF], F32))

        wqkv_sb = sb("wqkv_sb", [P, DC, 3 * D])
        wout_sb = sb("wout_sb", [P, DC, D])
        wq_sb = sb("wq_sb", [P, DC, D])
        wdkv_sb = sb("wdkv_sb", [P, DC, LAT])
        wuk_sb = sb("wuk_sb", [P, D])
        wuv_sb = sb("wuv_sb", [P, D])
        wo_sb = sb("wo_sb", [P, DC, D])
        gate_sb = sb("gate_sb", [P, DC, EXPERTS])
        bout_sb = sb("bout_sb", [P, D])
        gate_b_sb = sb("gate_b_sb", [P, EXPERTS])
        norms_sb = sb("norms_sb", [P, 2, DC])
        ln_sb = sb("ln_sb", [P, 2])
        perm_sb = sb("perm_sb", [P, 2, P])
        idf = sb("idf", [P, P])
        idb = sb("idb", [P, P], BF16)
        mask_sb = sb("mask_sb", [P, 2, P], BF16)
        table_sb = sb("table_sb", [P, 2, T])

        xs = sb("xs", [P, TT, D])
        y0 = sb("y0", [P, TT, D])
        xn = sb("xn", [P, TT, D])
        zs = sb("zs", [P, TT, D])
        xt = sb("xt", [P, DC, T])
        tmp = sb("tmp", [P, 4 * T])
        qs = [tmp[:, 0:T], tmp[:, T:2 * T]]
        y0t = tmp[:, 0:DC * T].rearrange("p (c n) -> p c n", c=DC)
        cosq = tmp[:, 2 * T:3 * T]
        rot = tmp[:, 3 * T:4 * T]
        rest = sb("rest", [P, T])
        parts = sb("parts", [P, 2, PARTS, T], BF16)
        vs = [sb(f"vs{a}", [P, TT, HEADS, HD + 1]) for a in range(2)]
        plain = sb("plain", [P, 2, 2, GROUP * T], BF16)
        turned = sb("turned", [P, 2, 2, GROUP * T], BF16)
        x_plain = plain[:, 0, 0, :].bitcast(F32).rearrange("p (t d) -> p t d", t=TT)
        prob = sb("prob", [P, 2, GROUP * HALF])
        o_sb = sb("o_sb", [P, 2, HALF])
        sums = sb("sums", [P, TT, HEADS])
        recip = sb("recip", [P, 16])
        stats = sb("stats", [P, TT, 6])
        mv = sb("mv", [P, TT, 2])
        t8 = sb("t8", [P, 6, TT])
        xn_flat = xn[:].rearrange("p t d -> p (t d)")
        latn, latt = xn_flat[:, 0:T], xn_flat[:, T:2 * T]
        maxes = sb("maxes", [P, GROUP * TT])
        mrow = sb("mrow", [GROUP * TT, 2, P])
        mpart = sb("mpart", [GROUP * TT, PARTS, P], BF16)
        logits = sb("logits", [P, TT, EXPERTS])
        top = sb("top", [P, TT])
        onehot = sb("onehot", [P, TT, EXPERTS])

        s_const = sem("s_const")
        values_padded = sem("values_padded")
        ones_written = sem("ones_written")
        slot_filled = [sem(f"slot_filled{i}") for i in range(SLOTS)]
        slot_drained = [sem(f"slot_drained{i}") for i in range(SLOTS)]
        v_step = sem("v_step")
        x_landed = sem("x_landed")
        residual_landed = sem("residual_landed")
        table_landed = sem("table_landed")
        normed = sem("normed")
        bias_added = sem("bias_added")
        cos_done = sem("cos_done")
        rot_done = sem("rot_done")
        split_done = sem("split_done")
        onehot_ready = sem("onehot_ready")
        parts_out = [sem(f"parts_out{i}") for i in range(2)]
        stack_in = [sem(f"stack_in{i}") for i in range(2)]
        pv_done = sem("pv_done")
        o_drained = sem("o_drained")
        t_filled = sem("t_filled")
        t_drained = sem("t_drained")
        max_split = sem("max_split")
        max_out = sem("max_out")
        max_in = [sem(f"max_in{i}") for i in range(2)]
        rows_out = sem("rows_out")
        in_loop = ([v_step, x_landed, residual_landed, table_landed, normed, bias_added,
                    cos_done, rot_done, split_done, onehot_ready, pv_done, o_drained, t_filled, t_drained,
                    max_split, max_out, rows_out] + slot_filled + slot_drained + parts_out + stack_in + max_in)

        consts = [(wqkv_sb, wqkv), (idf, ident_f), (idb, ident_b), (mask_sb, mask_b), (perm_sb, perm)]
        late_consts = [(wout_sb, wout), (wq_sb, wq), (wdkv_sb, wdkv), (wuk_sb, wuk), (wuv_sb, wuv), (wo_sb, wo),
                       (gate_sb, gate), (bout_sb, bout), (gate_b_sb, gate_b), (norms_sb, norms), (ln_sb, lnp)]
        with nc.Block(no_gpsimd_drain=True) as block:
            @block.sync
            def _(sp):
                for dst, src in consts:
                    sp.dma_start(dst[:], src).then_inc(s_const, 16)
                sp.wait_ge(s_const, 16 * len(consts))

            @block.vector
            def _(dve):
                for a in range(2):
                    nc.vector.memset(vs[a][:, :, :, HD:HD + 1], 1.0).then_inc(values_padded, 1)
                nc.vector.memset(o_bank[:], 0.0).then_inc(values_padded, 1)
                for tensor in (xn, zs):
                    nc.vector.memset(tensor[:], 0.0).then_inc(values_padded, 1)
                dve.wait_ge(values_padded, 5)

            @block.gpsimd
            def _(pool):
                for par in range(2):
                    nc.gpsimd.memset(turned[STACK:STACK + PARTS, par, 1, :], 1.0).then_inc(ones_written, 1)
                pool.wait_ge(ones_written, 2)

        def run(items, b, starts=False):
            plan = Plan(items)
            xin = xs if starts else x_plain

            def filled(eng, key):
                n = plan.slot[key]
                eng.wait_ge(slot_filled[n % SLOTS], n // SLOTS + 1)
                return slots[n % SLOTS]

            def wait_drained(eng, key):
                n = plan.slot[key]
                eng.wait_ge(slot_drained[n % SLOTS], n // SLOTS + 1)

            def drained(key):
                return slot_drained[plan.slot[key] % SLOTS]

            def wait_normed(eng, which, q):
                eng.wait_ge(normed, plan.normed[("norm", which, 1, q)] + 1)

            def x_of(q):
                return x[bass.ds(b + q, 1)].rearrange("b (t p) d -> p (b t) d", p=P)

            def unit_before(n):
                return next(k for k, m in plan.unit.items() if m == n - 2)

            with nc.Block(no_gpsimd_drain=True) as block:
                @block.sync
                def _(sp):
                    def load_stack(dst, row, g, side, par):
                        h0 = GROUP * g
                        at = 0
                        for term in ([[0, 1, 2], [0, 1], [0]] if side == 0 else [[0], [0], [0], [1], [1], [2]]):
                            n = len(term) * HD
                            src = scratch[row, h0:h0 + GROUP, term[0]:term[-1] + 1].rearrange("h t d n -> (t d) h n")
                            sp.dma_start(dst[at:at + n, :].rearrange("p (h n) -> p h n", h=GROUP),
                                         src).then_inc(stack_in[par], 16)
                            at += n

                    out_count = [0, 0]
                    for item in items:
                        kind, q = item[0], item[-1]
                        if kind == "getx":
                            prior = plan.last_before(lambda k: k[0] == "pv" and k[1] == 0, item)
                            if prior:
                                sp.wait_ge(pv_done, plan.pv[prior] + 1)
                            turn = plan.last_before(lambda k: k[0] == "turn" and k[1] == "xt0", item)
                            if turn:
                                filled(sp, turn)
                            sp.dma_start(xin[:, :, :], x_of(q)).then_inc(x_landed, 16)
                        elif kind == "residual":
                            if plan.last_before(lambda k: k[0] == "rows", item):
                                sp.wait_ge(rows_out, 48)
                            sp.dma_start(xs[:], x_of(q)).then_inc(residual_landed, 16)
                        elif kind == "table":
                            prior = plan.last_before(lambda k: k[0] == "cosine", item)
                            if prior:
                                sp.wait_ge(rot_done, plan.cosine[prior] + 1)
                            sp.dma_start(table_sb[:, 0, :], cos[item[1]]).then_inc(table_landed, 16)
                            sp.dma_start(table_sb[:, 1, :], sin[item[1]]).then_inc(table_landed, 16)
                        elif kind == "parts":
                            a, u, rotated = item[1:4]
                            tensor, blk = UNITS[u]
                            job = plan.job_of(a, u, rotated, q)
                            row = 4 * a + 2 * rotated * (1 - a) + (tensor == "k")
                            sp.wait_ge(split_done, job + 1)
                            for g in range(GROUPS):
                                last = plan.last_before(lambda k: k[0] == "group" and k[1:3] == (a, g), item)
                                if last and last[3] != q:
                                    sp.wait_ge(stack_in[g % 2], 16 * plan.stacked[last[1:]])
                            for t in range(PARTS):
                                sp.dma_start(scratch[row, 8 * blk:8 * blk + 8, t],
                                             parts[:, job % 2, t, :]).then_inc(parts_out[job % 2], 16)
                            out_count[job % 2] += 16 * PARTS
                        elif kind == "group":
                            if starts and item == ("group", 0, 2, 0):
                                for dst, src in late_consts:
                                    sp.dma_start(dst[:], src).then_inc(s_const, 16)
                            a, g = item[1:3]
                            par = g % 2
                            prior = plan.last_before(lambda k: k[0] == "pv" and k[2] // NSTEP % 2 == par
                                                     and k[2] % NSTEP == NSTEP - 2, item)
                            if prior:
                                sp.wait_ge(pv_done, plan.pv[prior] + 1)
                            for i in range(2):
                                if out_count[i]:
                                    sp.wait_ge(parts_out[i], out_count[i])
                            if a == 0:
                                turn = plan.last_before(lambda k: k[0] == "turn" and k[1] == "xt0", item)
                                if turn and par == 0:
                                    filled(sp, turn)
                                for side in range(2):
                                    load_stack(plain[:, par, side], side, g, side, par)
                            for side in range(2):
                                load_stack(turned[:, par, side], 2 + 2 * a + side, g, side, par)
                        elif kind == "maxrow":
                            g = item[1]
                            par = g % 2
                            n = plan.mx[("mx", 1, g, q)]
                            sp.wait_ge(max_split, n + 1)
                            for t in range(PARTS):
                                sp.dma_start(max_scratch[par, t].rearrange("j (r n) -> (j r) n", n=P),
                                             mpart[:, t, :]).then_inc(max_out, 16)
                            sp.wait_ge(max_out, 16 * PARTS * (n + 1))
                            sp.dma_start(turned[STACK:STACK + PARTS, par, 0, :].rearrange("p (h n) -> p h n", h=GROUP),
                                         max_scratch[par]).then_inc(max_in[par], 16)
                        elif kind == "rows":
                            rows_q = rows[0:(B + 1) * T].rearrange("(b t p) c -> b p t c", b=B + 1, p=P)
                            rows_q = rows_q[bass.ds(b + q + 1, 1)].rearrange("b p t c -> (b p) t c")
                            wait_normed(sp, 2, q)
                            sp.dma_start(rows_q[:, :, 0:D], xn[:]).then_inc(rows_out, 16)
                            sp.wait_ge(onehot_ready, plan.pick[("pick", q)] + 1)
                            sp.dma_start(chosen[bass.ds(b + q + 1, 1)].rearrange("b p t e -> (b p) t e"),
                                         onehot[:]).then_inc(rows_out, 16)
                            sp.dma_start(rows_q[:, :, D:2 * D], xs[:]).then_inc(rows_out, 16)
                    if starts:
                        sp.wait_ge(s_const, 16 * (len(consts) + len(late_consts)))
                    for i in range(2):
                        if out_count[i]:
                            sp.wait_ge(parts_out[i], out_count[i])
                        if plan.stack_total[i]:
                            sp.wait_ge(stack_in[i], 16 * plan.stack_total[i])
                        if plan.max_total[i]:
                            sp.wait_ge(max_in[i], 16 * plan.max_total[i])
                    if plan.rows:
                        sp.wait_ge(rows_out, 48 * len(plan.rows))
                    if plan.getx:
                        sp.wait_ge(x_landed, 16 * len(plan.getx))
                    if plan.residual:
                        sp.wait_ge(residual_landed, 16 * len(plan.residual))
                    if plan.table:
                        sp.wait_ge(table_landed, 32 * len(plan.table))

                @block.tensor
                def _(pe):
                    def take(key):
                        n = plan.slot[key]
                        if n >= SLOTS:
                            pe.wait_ge(slot_drained[n % SLOTS], n // SLOTS)
                        return slots[n % SLOTS]

                    def give(key, ins):
                        ins.then_inc(slot_filled[plan.slot[key] % SLOTS], 1)

                    def turn(key):
                        what, c, q = key[1:]
                        if what == "xt0":
                            wait_normed(pe, 0, q)
                            src = lambda t: xin[:, t, c * P:(c + 1) * P]
                        elif what == "yt0":
                            src = lambda t: y0[:, t, c * P:(c + 1) * P]
                        elif what == "lt":
                            wait_normed(pe, 3, q)
                            src = lambda t: latn[:, t * P:(t + 1) * P]
                        else:
                            if what == "xt1":
                                wait_normed(pe, 1, q)
                            elif what == "xt2":
                                wait_normed(pe, 2, q)
                            else:
                                last_ot = plan.last_before(lambda k: k[0] == "ot" and k[1] == 1, key)
                                if last_ot:
                                    pe.wait_ge(t_drained, plan.bank[last_ot] + 1)
                            src = lambda t: xn[:, t, c * P:(c + 1) * P]
                        slot = take(key)
                        for t in range(TT):
                            last = nc.tensor.transpose(slot[:, t * P:(t + 1) * P], src(t), idf[:])
                        give(key, last)

                    def project(key):
                        a, u, q = key[1:]
                        tensor, blk = UNITS[u]
                        if a == 1 and tensor == "k":
                            wait_drained(pe, ("turn", "lt", 0, q))
                        else:
                            for c in range(DC):
                                wait_drained(pe, ("turn", f"xt{a}", c, q))
                        slot = take(key)
                        for half in range(2):
                            cols = slice(half * HALF, (half + 1) * HALF)
                            if a == 1 and tensor == "k":
                                pairs = [(wuk_sb[:, blk * P:(blk + 1) * P], latt[:, cols])]
                            elif a == 1:
                                pairs = [(wq_sb[:, c, blk * P:(blk + 1) * P], xt[:, c, cols]) for c in range(DC)]
                            else:
                                at = (tensor == "k") * D + blk * P
                                pairs = [(wqkv_sb[:, c, at:at + P], xt[:, c, cols]) for c in range(DC)]
                            for c, (w, r) in enumerate(pairs):
                                last = nc.tensor.matmul(slot[:, cols], w, r, start=c == 0, stop=c == len(pairs) - 1)
                        give(key, last)

                    def swap(key):
                        a, u, q = key[1:]
                        wait_drained(pe, ("proj", a, u, q))
                        slot = take(key)
                        for half in range(2):
                            cols = slice(half * HALF, (half + 1) * HALF)
                            last = nc.tensor.matmul(slot[:, cols], perm_sb[:, a, :], qs[plan.swap[key] % 2][:, cols],
                                                    start=True, stop=True)
                        give(key, last)

                    def token_rows(key, l, w, width):
                        slot = take(key)
                        per = 2 * HALF // width
                        first = per * key[-2] if isinstance(key[-2], int) else 0
                        for i in range(per):
                            n = len(w)
                            for c in range(n):
                                last = nc.tensor.matmul(slot[:, i * width:(i + 1) * width], l(c, first + i), w[c],
                                                        start=c == 0, stop=c == n - 1)
                        give(key, last)

                    def channels(c, t):
                        return xt[:, c, t * P:(t + 1) * P]

                    def head(buf, par, side, j, rows_):
                        return buf[0:rows_, par, side, j * T:(j + 1) * T]

                    for item in items:
                        kind, q = item[0], item[-1]
                        if kind == "turn":
                            turn(item)
                        elif kind == "proj":
                            project(item)
                        elif kind == "swap":
                            swap(item)
                        elif kind == "v":
                            if item[1] == 0:
                                token_rows(item, channels, [wqkv_sb[:, c, 2 * D:3 * D] for c in range(DC)], D)
                            else:
                                wait_drained(pe, ("turn", "lt", 0, q))
                                token_rows(item, lambda c, t: latt[:, t * P:(t + 1) * P], [wuv_sb[:]], D)
                        elif kind == "op":
                            a = item[1]
                            for c in range(DC):
                                wait_drained(pe, ("turn", f"yt{a}", c, q))
                            if a == 0:
                                token_rows(item, lambda c, t: y0t[:, c, t * P:(t + 1) * P],
                                           [wout_sb[:, c, :] for c in range(DC)], D)
                            else:
                                token_rows(item, channels, [wo_sb[:, c, :] for c in range(DC)], D)
                        elif kind == "lat":
                            for c in range(DC):
                                wait_drained(pe, ("turn", "xt1", c, q))
                            token_rows(item, channels, [wdkv_sb[:, c, :] for c in range(DC)], LAT)
                        elif kind == "gate":
                            for c in range(DC):
                                wait_drained(pe, ("turn", "xt2", c, q))
                            slot = take(item)
                            for t in range(TT):
                                for c in range(DC):
                                    last = nc.tensor.matmul(slot[:, t * EXPERTS:(t + 1) * EXPERTS], channels(c, t),
                                                            gate_sb[:, c, :], start=c == 0, stop=c == DC - 1)
                            give(item, last)
                        elif kind == "num":
                            a, s, part = item[1:4]
                            g, i = divmod(s, NSTEP)
                            half, kb, lo, w = STEPS[i]
                            heads = GROUP // SCORE_SLOTS[i]
                            diagonal = lo == kb * P
                            rows_ = STACK + PARTS * a
                            if i == 0 and part == 0:
                                if a == 0 and (a, g, q) in plan.stacked:
                                    pe.wait_ge(stack_in[g % 2], 16 * plan.stacked[(a, g, q)])
                                elif a == 1:
                                    pe.wait_ge(max_in[g % 2], 16 * plan.maxed[(g, q)])
                                if s == 0:
                                    for h in range(2):
                                        if ("v", a, h, q) in plan.slot:
                                            wait_drained(pe, ("v", a, h, q))
                            slot = take(item)
                            for k in range(heads):
                                j = heads * part + k
                                at = k * (2 * HALF // heads)
                                dst = slot[:, at:at + w]
                                last = nc.tensor.matmul(
                                    dst, head(turned, g % 2, 1, j, rows_)[:, kb * P:(kb + 1) * P],
                                    head(turned, g % 2, 0, j, rows_)[:, lo:lo + w], start=True, stop=not diagonal)
                                if diagonal:
                                    last = nc.tensor.matmul(dst[:, 0:P], idb[:], mask_sb[:, 0, :],
                                                            start=False, stop=True)
                            give(item, last)
                        elif kind == "den":
                            g, j, qb = item[2:5]
                            slot = take(item)
                            for half in range(2):
                                cols = slice(half * HALF, (half + 1) * HALF)
                                last = nc.tensor.matmul(slot[:, cols], head(plain, g % 2, 0, j, STACK)[:, qb * P:(qb + 1) * P],
                                                        head(plain, g % 2, 1, j, STACK)[:, cols], start=True, stop=True)
                            give(item, last)
                        elif kind == "max":
                            g, j, qb = item[2:5]
                            if j == 0 and qb == 0:
                                pe.wait_ge(stack_in[g % 2], 16 * plan.stacked[(1, g, q)])
                            slot = take(item)
                            w = (qb + 1) * P
                            for k in range(2 if w <= HALF else 1):
                                lhs = head(turned, g % 2, 0, j + k, STACK)[:, qb * P:(qb + 1) * P]
                                for at in range(0, w, HALF):
                                    end = min(at + HALF, w)
                                    nc.tensor.matmul(slot[:, k * HALF + at:k * HALF + end], lhs,
                                                     head(turned, g % 2, 1, j + k, STACK)[:, at:end],
                                                     start=True, stop=end < w)
                                last = nc.tensor.matmul(slot[:, k * HALF + w - P:k * HALF + w], idb[:],
                                                        mask_sb[:, 1, :], start=False, stop=True)
                            give(item, last)
                        elif kind == "pv":
                            a, s = item[1:3]
                            g, i = divmod(s, NSTEP)
                            half, kb, lo, w = STEPS[i]
                            for k in range(SCORE_SLOTS[i]):
                                wait_drained(pe, ("num", a, s, k, q))
                            n = sum(m < plan.pv[item] for m in (plan.pv[k] for k in plan.half))
                            if kb == 0 and n >= 1:
                                pe.wait_ge(o_drained, n)
                            for j in range(GROUP):
                                last = nc.tensor.matmul(
                                    o_bank[32 * j:32 * j + HD + 1, lo - half * HALF:HALF],
                                    vs[a][:, kb, GROUP * g + j, :],
                                    prob[:, plan.pv[item] % 2, j * HALF:j * HALF + w],
                                    start=kb == 0, stop=closes(s), tile_position=(0, 32 * j))
                            last.then_inc(pv_done, 1)
                        elif kind == "ot":
                            a, g, half = item[1:4]
                            n = plan.half[("pv", a, NSTEP * g + (3 if half == 0 else NSTEP - 1), q)]
                            pe.wait_ge(o_drained, n + 1)
                            if plan.bank[item] >= 1:
                                pe.wait_ge(t_drained, plan.bank[item])
                            for i in range(4):
                                last = nc.tensor.transpose(t_bank[:, i * P:(i + 1) * P],
                                                           o_sb[:, n % 2, i * P:(i + 1) * P], idf[:])
                            last.then_inc(t_filled, 1)
                        elif kind == "mx":
                            wait_drained(pe, ("max", 1, item[2], GROUP - 1, TT - 1, q))
                            if plan.bank[item] >= 1:
                                pe.wait_ge(t_drained, plan.bank[item])
                            nc.tensor.transpose(t_bank[0:GROUP * TT, 0:P], maxes[:, :], idf[:]).then_inc(t_filled, 1)

                @block.scalar
                def _(act):
                    for item in items:
                        kind, q = item[0], item[-1]
                        if starts and kind in ("turn", "proj", "v"):
                            continue
                        if kind == "turn" and item[1] == "xt0":
                            slot = filled(act, item)
                            nc.scalar.activation(xt[:, item[2], :], slot[:], ACT.Copy).then_inc(drained(item), 1)
                        elif kind == "proj" and item[1] == 0:
                            n = plan.unit[item]
                            if n >= 2:
                                _, a2, u2, q2 = unit_before(n)
                                filled(act, ("swap", a2, u2, q2))
                                act.wait_ge(cos_done, n - 1)
                                if a2 == 0:
                                    act.wait_ge(split_done, plan.job_of(0, u2, 0, q2) + 1)
                            slot = filled(act, item)
                            nc.scalar.activation(qs[n % 2], slot[:], ACT.Copy).then_inc(drained(item), 1)
                        elif kind == "v" and item[1] == 0:
                            h = item[2]
                            slot = filled(act, item)
                            nc.scalar.activation(vs[0][:, 4 * h:4 * h + 4, :, 0:HD],
                                                 slot[:].rearrange("p (t h d) -> p t h d", t=4, h=HEADS),
                                                 ACT.Copy).then_inc(drained(item), 1)
                        elif kind == "num":
                            s, part = item[2:4]
                            heads = GROUP // SCORE_SLOTS[s % NSTEP]
                            w = STEPS[s % NSTEP][3]
                            n = plan.pv[("pv", item[1], s, q)]
                            if part == 0 and n >= 2:
                                act.wait_ge(pv_done, n - 1)
                            slot = filled(act, item)
                            dst = prob[:, n % 2, heads * part * HALF:heads * (part + 1) * HALF]
                            nc.scalar.activation(dst.rearrange("p (h n) -> p h n", h=heads)[:, :, 0:w],
                                                 slot[:].rearrange("p (h n) -> p h n", h=heads)[:, :, 0:w],
                                                 ACT.Exp, scale=SCALE).then_inc(drained(item), 1)
                        elif kind == "den":
                            g, j, qb = item[2:5]
                            slot = filled(act, item)
                            h = GROUP * g + j
                            nc.scalar.activation(slot[:], slot[:], ACT.Exp, scale=SCALE,
                                                 accum_out=sums[:, qb, h:h + 1]).then_inc(drained(item), 1)

                        elif kind == "pv" and closes(item[2]) and item[1] == 1:
                            n = plan.half[item]
                            act.wait_ge(pv_done, plan.pv[item] + 1)
                            if n >= 2:
                                last = plan.last_before(lambda k: k[0] == "ot", item)
                                before = plan.last_before(lambda k: k[0] == "ot", last) or last
                                act.wait_ge(t_filled, plan.bank[before] + 1)
                            nc.scalar.activation(o_sb[:, n % 2, :], o_bank[:], ACT.Copy).then_inc(o_drained, 1)

                @block.gpsimd
                def _(pool):
                    for item in items:
                        kind, q = item[0], item[-1]
                        if kind == "residual":
                            pool.wait_ge(residual_landed, 16 * (plan.residual[item] + 1))
                            nc.gpsimd.tensor_tensor(xs[:], xs[:], bout_sb[:].unsqueeze(1).to_broadcast([P, TT, D]),
                                                    ALU.add).then_inc(bias_added, 1)
                        elif kind == "proj":
                            n = plan.unit[item]
                            wait_drained(pool, item)
                            tables = plan.last_before(lambda k: k[0] == "table", item)
                            pool.wait_ge(table_landed, 32 * (plan.table[tables] + 1))
                            if n >= 1:
                                pool.wait_ge(rot_done, n)
                            nc.gpsimd.tensor_tensor(cosq, qs[n % 2], table_sb[:, 0, :], ALU.mult).then_inc(cos_done, 1)

                @block.vector
                def _(dve):
                    steps = [0]

                    def link(ins):
                        steps[0] += 1
                        ins.then_inc(v_step, 1)
                        dve.wait_ge(v_step, steps[0])

                    def token_stats(which, part, q):
                        if which == 0 and part == 0:
                            dve.wait_ge(x_landed, 16 * (plan.getx[("getx", q)] + 1))
                        src = {0: lambda t: xin[:, t, :], 1: lambda t: xs[:, t, :], 2: lambda t: zs[:, t, :],
                               3: lambda t: latn[:, t * P:(t + 1) * P]}[which]
                        for t in range(4 * part, 4 * part + 4):
                            ins = nc.vector.bn_stats(stats[:, t, :], src(t))
                        link(ins)
                        for t in range(4 * part, 4 * part + 4):
                            ins = nc.vector.bn_aggr(mv[:, t, :], stats[:, t, :])
                        link(ins)

                    def root(item):
                        which = item[1]
                        eps = 1e-6 if which in (2, 4) else 1e-5
                        if which == 4:
                            link(nc.vector.tensor_tensor(t8[:, 3, :], mv[:, :, 1], t8[:, 2, :], ALU.mult))
                            link(nc.vector.tensor_tensor(t8[:, 3, :], t8[:, 3, :], t8[:, 2, :], ALU.mult))
                            src = t8[:, 3, :]
                        elif which == 2:
                            link(nc.vector.tensor_tensor(t8[:, 3, :], mv[:, :, 0], mv[:, :, 0], ALU.mult))
                            link(nc.vector.tensor_tensor(t8[:, 3, :], t8[:, 3, :], mv[:, :, 1], ALU.add))
                            src = t8[:, 3, :]
                        else:
                            src = mv[:, :, 1]
                        dst = t8[:, 4 if which in (2, 4) else 2, :]
                        a, h = t8[:, 0, :], t8[:, 5, :]
                        link(nc.vector.tensor_scalar(a, src, eps, None, ALU.add))
                        nc.vector.tensor_scalar(h, a, -0.5, None, ALU.mult)
                        link(nc.vector.tensor_scalar(t8[:, 1, :].bitcast(I32), a.bitcast(I32), 1, None,
                                                     ALU.logical_shift_right))
                        link(nc.vector.tensor_scalar(dst.bitcast(I32), t8[:, 1, :].bitcast(I32), -1.0,
                                                     float(ROOT_GUESS), ALU.mult, ALU.add))
                        for _ in range(3):
                            link(nc.vector.tensor_tensor(a, dst, dst, ALU.mult))
                            link(nc.vector.tensor_tensor(a, a, h, ALU.mult))
                            link(nc.vector.scalar_tensor_tensor(out=dst, in0=a, scalar=1.5, in1=dst,
                                                                op0=ALU.add, op1=ALU.mult))

                    def norm(item):
                        which, part, q = item[1:]
                        tiles = range(4 * part, 4 * part + 4)
                        if which == 0:
                            for t in tiles:
                                ins = nc.vector.tensor_scalar(xin[:, t, :], xin[:, t, :], mv[:, t, 0:1],
                                                              t8[:, 2, t:t + 1], ALU.subtract, ALU.mult)
                        elif which == 1:
                            for t in tiles:
                                ins = nc.vector.tensor_scalar(zs[:, t, :], xs[:, t, :], mv[:, t, 0:1],
                                                              t8[:, 2, t:t + 1], ALU.subtract, ALU.mult)
                            link(ins)
                            if part == 0 and plan.last_before(lambda k: k[0] == "rows", item):
                                dve.wait_ge(rows_out, 48)
                            for t in tiles:
                                ins = nc.vector.tensor_scalar(xn[:, t, :], zs[:, t, :], t8[:, 4, t:t + 1], None, ALU.mult)
                        elif which == 2:
                            for t in tiles:
                                ins = nc.vector.tensor_scalar(xn[:, t, :], zs[:, t, :], t8[:, 4, t:t + 1], None, ALU.mult)
                        else:
                            for t in range(TT):
                                ins = nc.vector.tensor_scalar(latn[:, t * P:(t + 1) * P], latn[:, t * P:(t + 1) * P],
                                                              mv[:, t, 0:1], t8[:, 2, t:t + 1], ALU.subtract, ALU.mult)
                        if part == 1:
                            ins.then_inc(normed, 1)
                            wait_normed(dve, which, q)
                        else:
                            link(ins)

                    def split(item):
                        a, u, rotated, second, q = item[1:]
                        job = plan.job_of(a, u, rotated, q)
                        n = plan.unit[("proj", a, u, q)]
                        par = job % 2
                        src = rot if rotated else qs[n % 2]
                        if not second:
                            if not rotated:
                                wait_drained(dve, ("proj", a, u, q))
                            if job >= 2:
                                dve.wait_ge(parts_out[par], 16 * PARTS * (job // 2))
                            link(nc.vector.tensor_copy(parts[:, par, 0, :], src))
                            link(nc.vector.tensor_tensor(rest[:], src, parts[:, par, 0, :], ALU.subtract))
                        else:
                            link(nc.vector.tensor_copy(parts[:, par, 1, :], rest[:]))
                            nc.vector.tensor_tensor(parts[:, par, 2, :], rest[:], parts[:, par, 1, :],
                                                    ALU.subtract).then_inc(split_done, 1)
                            dve.wait_ge(split_done, job + 1)

                    for item in items:
                        kind, q = item[0], item[-1]
                        if kind == "stat":
                            token_stats(item[1], item[2], q)
                        elif kind == "root":
                            root(item)
                        elif kind == "norm":
                            norm(item)
                        elif kind == "turn" and (item[1] != "xt0" or starts):
                            what, c = item[1:3]
                            slot = filled(dve, item)
                            if what == "lt":
                                ins = nc.vector.tensor_scalar(latt, slot[:], ln_sb[:, 0:1], ln_sb[:, 1:2], ALU.mult, ALU.add)
                            elif what in ("xt1", "xt2"):
                                ins = nc.vector.tensor_scalar(xt[:, c, :], slot[:], norms_sb[:, int(what[2]) - 1, c:c + 1],
                                                              None, ALU.mult)
                            else:
                                dst = y0t if what == "yt0" else xt
                                ins = nc.vector.tensor_copy(dst[:, c, :], slot[:])
                            ins.then_inc(drained(item), 1)
                        elif kind == "lat":
                            slot = filled(dve, item)
                            nc.vector.tensor_copy(latn, slot[:]).then_inc(drained(item), 1)
                            wait_drained(dve, item)
                        elif kind == "proj" and (item[1] == 1 or starts):
                            n = plan.unit[item]
                            if n >= 2:
                                filled(dve, ("swap", *unit_before(n)[1:]))
                                dve.wait_ge(cos_done, n - 1)
                            slot = filled(dve, item)
                            nc.vector.tensor_copy(qs[n % 2], slot[:]).then_inc(drained(item), 1)
                        elif kind == "sine":
                            key = ("swap", *item[1:])
                            tables = plan.last_before(lambda k: k[0] == "table", item)
                            dve.wait_ge(table_landed, 32 * (plan.table[tables] + 1))
                            slot = filled(dve, key)
                            nc.vector.tensor_tensor(rot, slot[:], table_sb[:, 1, :], ALU.mult).then_inc(drained(key), 1)
                        elif kind == "cosine":
                            wait_drained(dve, ("swap", *item[1:]))
                            n = plan.cosine[item]
                            dve.wait_ge(cos_done, n + 1)
                            nc.vector.tensor_tensor(rot, rot, cosq, ALU.add).then_inc(rot_done, 1)
                            dve.wait_ge(rot_done, n + 1)
                        elif kind == "split":
                            split(item)
                        elif kind == "v" and (item[1] == 1 or starts):
                            a, h = item[1:3]
                            slot = filled(dve, item)
                            nc.vector.tensor_copy(vs[a][:, 4 * h:4 * h + 4, :, 0:HD],
                                                  slot[:].rearrange("p (t h d) -> p t h d", t=4, h=HEADS)
                                                  ).then_inc(drained(item), 1)
                        elif kind == "op":
                            h = item[2]
                            if item[1] == 0 and h == 0:
                                dve.wait_ge(bias_added, plan.residual[("residual", q)] + 1)
                            dst = zs if item[1] == 1 else xs
                            slot = filled(dve, item)
                            part = dst[:, 4 * h:4 * h + 4, :].rearrange("p t d -> p (t d)")
                            nc.vector.tensor_tensor(part, slot[:], part, ALU.add).then_inc(drained(item), 1)
                            wait_drained(dve, item)
                        elif kind == "sum":
                            link(nc.vector.tensor_tensor(xs[:], xs[:], zs[:], ALU.add))
                        elif kind == "gate":
                            slot = filled(dve, item)
                            nc.vector.tensor_tensor(logits[:], slot[:, 0:TT * EXPERTS].rearrange("p (t e) -> p t e", e=EXPERTS),
                                                    gate_b_sb[:].unsqueeze(1).to_broadcast([P, TT, EXPERTS]),
                                                    ALU.add).then_inc(drained(item), 1)
                            wait_drained(dve, item)
                        elif kind == "pick":
                            link(nc.vector.reduce_max(top[:], logits[:], AX_X))
                            link(nc.vector.tensor_tensor(onehot[:], logits[:],
                                                         top[:].unsqueeze(2).to_broadcast([P, TT, EXPERTS]), ALU.is_ge))
                            link(nc.vector.tensor_copy(top[:], onehot[:, :, 0]))
                            for e in range(1, EXPERTS):
                                ins = nc.vector.tensor_tensor(onehot[:, :, e], onehot[:, :, e], top[:], ALU.is_gt)
                                if e < EXPERTS - 1:
                                    link(ins)
                                    link(nc.vector.tensor_tensor(top[:], top[:], onehot[:, :, e], ALU.max))
                            ins.then_inc(onehot_ready, 1)
                            dve.wait_ge(onehot_ready, plan.pick[item] + 1)
                        elif kind == "max":
                            g, j, qb = item[2:5]
                            slot = filled(dve, item)
                            prior = plan.last_before(lambda k: k[0] == "mx", item)
                            if prior and j == 0 and qb == 0:
                                dve.wait_ge(t_filled, plan.bank[prior] + 1)
                            w = (qb + 1) * P
                            heads = 2 if w <= HALF else 1
                            nc.vector.reduce_max(maxes[:].rearrange("p (j t) -> p j t", t=TT)[:, j:j + heads, qb],
                                                 slot[:].rearrange("p (h n) -> p h n", h=heads)[:, :, 0:w],
                                                 AX_X).then_inc(drained(item), 1)
                        elif kind == "mx":
                            n = plan.mx[item]
                            dve.wait_ge(t_filled, plan.bank[item] + 1)
                            if n >= 1:
                                dve.wait_ge(max_out, 16 * PARTS * n)
                            nc.vector.tensor_scalar(mrow[:, 0, :], t_bank[0:GROUP * TT, 0:P], -1.0, None,
                                                    ALU.mult).then_inc(t_drained, 1)
                            dve.wait_ge(t_drained, plan.bank[item] + 1)
                            link(nc.vector.tensor_copy(mpart[:, 0, :], mrow[:, 0, :]))
                            link(nc.vector.tensor_tensor(mrow[:, 1, :], mrow[:, 0, :], mpart[:, 0, :], ALU.subtract))
                            link(nc.vector.tensor_copy(mpart[:, 1, :], mrow[:, 1, :]))
                            nc.vector.tensor_tensor(mpart[:, 2, :], mrow[:, 1, :], mpart[:, 1, :],
                                                    ALU.subtract).then_inc(max_split, 1)
                            dve.wait_ge(max_split, n + 1)
                        elif kind == "pv" and closes(item[2]) and item[1] == 0:
                            n = plan.half[item]
                            dve.wait_ge(pv_done, plan.pv[item] + 1)
                            nc.vector.tensor_copy(o_sb[:, n % 2, :], o_bank[:]).then_inc(o_drained, 1)
                        elif kind == "ot":
                            a, g, half = item[1:4]
                            rc = recip[:].rearrange("p (t h) -> p t h", t=4)
                            turned_o = t_bank[:].rearrange("p (t h c) -> p t h c", t=4, h=GROUP)
                            dve.wait_ge(t_filled, plan.bank[item] + 1)
                            if a == 0:
                                wait_drained(dve, ("den", 0, g, GROUP - 1, 4 * half + 3, q))
                                link(nc.vector.reciprocal(rc, sums[:, 4 * half:4 * half + 4, GROUP * g:GROUP * (g + 1)]))
                            else:
                                link(nc.vector.reciprocal(rc.unsqueeze(3), turned_o[:, :, :, HD:HD + 1]))
                            dst = (xn if a else y0)[:, 4 * half:4 * half + 4, :].rearrange("p t (h d) -> p t h d", h=HEADS)
                            nc.vector.tensor_tensor(dst[:, :, GROUP * g:GROUP * (g + 1), :], turned_o[:, :, :, 0:HD],
                                                    rc.unsqueeze(3).to_broadcast([P, 4, GROUP, HD]),
                                                    ALU.mult).then_inc(t_drained, 1)

            for s in in_loop:
                nc.sync.sem_clear(s)
            nc.all_engine_barrier()

        run(items_of_start(), 0, starts=True)
        with nc.Fori(0, B - 1, 1) as b:
            run(items_of_loop(), b)
        run(items_of_end(), B - 1)


def build_experts(nc, rows, chosen, norms, w1, b1, w2, b2, ident_f, before, starts, tile_ids, token_ids, no_token,
                  zero_row, out):
    table = nc.dram_tensor("token_of_slot", (P * TILES, 1), U32, kind="Internal").ap()
    out_rows = out.rearrange("b t d -> (b t) d")
    NT = B * TT
    with ExitStack() as ctx:
        def sb(name, shape, dt=F32):
            return ctx.enter_context(nc.sbuf_tensor(name, shape, dt))

        def sem(name):
            return ctx.enter_context(nc.semaphore(name))

        def pb(name, shape):
            return ctx.enter_context(nc.psum_tensor(name, shape, F32))

        h_ps = pb("h_ps", [P, HID])
        ht_ps = pb("ht_ps", [P, HC, P])
        y_ps = [pb(f"y_ps{i}", [P, HALF]) for i in range(2)]
        x_ps = [pb(f"x_ps{i}", [P, HALF]) for i in range(2)]

        w1_sb = sb("w1_sb", [P, EXPERTS, DC * HID])
        w2_sb = sb("w2_sb", [P, EXPERTS, HC * D])
        b1_sb = sb("b1_sb", [P, EXPERTS, HID])
        b2_sb = sb("b2_sb", [P, EXPERTS, D])
        norms_sb = sb("norms2_sb", [P, 2, DC])
        idf = sb("idf2", [P, P])
        before_sb = sb("before_sb", [P, 2, P])
        starts_sb = sb("starts_sb", [P, NT])
        tile_ids_sb = sb("tile_ids_sb", [P, TILES])
        token_ids_sb = sb("token_ids_sb", [P, NT], U32)
        oh = sb("oh", [P, NT, EXPERTS])
        upto = [sb(f"upto{i}", [P, NT, EXPERTS]) for i in range(2)]
        slot_of = sb("slot_of", [P, NT, EXPERTS])
        passed = sb("passed", [P, EXPERTS, NT])
        tiles = sb("tiles", [P, EXPERTS])
        ends = sb("ends", [P, EXPERTS])
        first = sb("first", [P, EXPERTS])
        slot_f = sb("slot_f", [P, NT])
        slot_i = sb("slot_i", [P, NT], I32)
        slot_lo = sb("slot_lo", [P, NT], I32)
        slot_hi = sb("slot_hi", [P, NT], I32)
        place = sb("place", [P, NT], U32)
        tile_expert_f = sb("tile_expert_f", [P, TILES])
        tile_expert = sb("tile_expert", [P, TILES], I32)
        tokens = sb("tokens", [P, TILES], U32)
        out_tokens = sb("out_tokens", [P, TILES], U32)
        now = sb("now", [P, UNROLL], U32)
        now_out = sb("now_out", [P, UNROLL], U32)
        xg = sb("xg", [P, GATHERED, 2 * D])
        xgt = sb("xgt", [P, 2, DC * P])
        hs = sb("hs", [P, 2, HID])
        hst = sb("hst", [P, 2, HC, P])
        yo = sb("yo", [P, GATHERED, D])

        s_const = sem("s_const2")
        w_landed = sem("w_landed")
        table_cleared = sem("table_cleared")
        ranked = sem("ranked")
        d_step = sem("d_step")
        placed = sem("placed")
        scattered = sem("scattered")
        tokens_in = sem("tokens_in")
        experts_ready = sem("experts_ready")
        now_ready = sem("now_ready")
        gathered = [sem(f"gathered{i}") for i in range(GATHERED)]
        stored = [sem(f"stored{i}") for i in range(GATHERED)]
        x_turned = sem("x_turned")
        x_drained = sem("x_drained")
        h_made = sem("h_made")
        h_drained = sem("h_drained")
        h_turned = sem("h_turned")
        ht_drained = sem("ht_drained")
        y_made = sem("y_made")
        y_based = sem("y_based")
        y_added = sem("y_added")

        consts = [(norms_sb, norms), (idf, ident_f), (before_sb, before), (starts_sb, starts),
                  (tile_ids_sb, tile_ids), (token_ids_sb, token_ids)]
        with nc.Block() as block:
            @block.sync
            def _(sp):
                for dst, src in consts:
                    sp.dma_start(dst[:], src).then_inc(s_const, 16)
                sp.dma_start(oh[:].rearrange("p (b t) e -> p b t e", b=B),
                             chosen[1:].rearrange("b p t e -> p b t e")).then_inc(s_const, 16)
                sp.dma_start(table.rearrange("(p t) o -> p (t o)", p=P), no_token).then_inc(table_cleared, 16)
                sp.dma_start(rows[(B + 1) * T:], zero_row).then_inc(table_cleared, 16)
                for e in range(EXPERTS):
                    sp.dma_start(w1_sb[:, e], w1[e]).then_inc(w_landed, 16)
                    sp.dma_start(w2_sb[:, e], w2[e]).then_inc(w_landed, 16)
                sp.dma_start(b1_sb[:], b1).then_inc(w_landed, 16)
                sp.dma_start(b2_sb[:], b2).then_inc(w_landed, 16)
                sp.wait_ge(scattered, 16 * NT)
                sp.dma_start(tokens[:], table.rearrange("(p t) o -> p (t o)", p=P)).then_inc(tokens_in, 16)
                sp.wait_ge(tokens_in, 16)

            @block.tensor
            def _(pe):
                pe.wait_ge(s_const, 16 * (len(consts) + 1))
                oh_flat = oh[:].rearrange("p t e -> p (t e)")
                nc.tensor.matmul(h_ps[:, 0:NT * EXPERTS], before_sb[:, 0, :], oh_flat, start=True, stop=True)
                nc.tensor.matmul(h_ps[:, HALF:HALF + NT * EXPERTS], before_sb[:, 1, :], oh_flat,
                                 start=True, stop=True).then_inc(ranked, 1)

            @block.vector
            def _(dve):
                steps = [0]

                def link(ins):
                    steps[0] += 1
                    ins.then_inc(d_step, 1)
                    dve.wait_ge(d_step, steps[0])

                dve.wait_ge(ranked, 1)
                rank = h_ps[:, 0:NT * EXPERTS].rearrange("p (t e) -> p t e", e=EXPERTS)
                total = h_ps[:, HALF:HALF + NT * EXPERTS].rearrange("p (t e) -> p t e", e=EXPERTS)
                a, z = upto
                link(nc.vector.tensor_copy(a[:], total))
                n = 1
                while n < NT:
                    nc.vector.tensor_copy(z[:, 0:n, :], a[:, 0:n, :])
                    link(nc.vector.tensor_tensor(z[:, n:, :], a[:, n:, :], a[:, 0:NT - n, :], ALU.add))
                    a, z = z, a
                    n *= 2
                link(nc.vector.tensor_tensor(passed[:], starts_sb[:].unsqueeze(1).to_broadcast([P, EXPERTS, NT]),
                                             a[:, NT - 1, :].unsqueeze(2).to_broadcast([P, EXPERTS, NT]), ALU.is_lt))
                link(nc.vector.reduce_sum(tiles[:], passed[:], AX_X))
                link(nc.vector.tensor_copy(ends[:], tiles[:]))
                for e in range(1, EXPERTS):
                    link(nc.vector.tensor_tensor(ends[:, e:e + 1], ends[:, e - 1:e], tiles[:, e:e + 1], ALU.add))
                link(nc.vector.tensor_tensor(first[:], ends[:], tiles[:], ALU.subtract))
                link(nc.vector.tensor_scalar(first[:], first[:], float(P), None, ALU.mult))
                link(nc.vector.tensor_tensor(slot_of[:], total, a[:], ALU.subtract))
                link(nc.vector.tensor_tensor(slot_of[:], rank, slot_of[:], ALU.subtract))
                link(nc.vector.tensor_tensor(slot_of[:], slot_of[:], first[:].unsqueeze(1).to_broadcast([P, NT, EXPERTS]),
                                             ALU.add))
                link(nc.vector.tensor_tensor(slot_of[:], slot_of[:], oh[:], ALU.mult))
                link(nc.vector.reduce_sum(slot_f[:], slot_of[:], AX_X))
                link(nc.vector.tensor_copy(slot_i[:], slot_f[:]))
                link(nc.vector.tensor_scalar(slot_lo[:], slot_i[:], P - 1, None, ALU.bitwise_and))
                link(nc.vector.tensor_scalar(slot_hi[:], slot_i[:], P.bit_length() - 1, None, ALU.logical_shift_right))
                nc.vector.scalar_tensor_tensor(out=place[:], in0=slot_lo[:], scalar=float(TILES), in1=slot_hi[:],
                                               op0=ALU.mult, op1=ALU.add).then_inc(placed, 1)
                link(nc.vector.tensor_scalar(tile_expert_f[:], tile_ids_sb[:], ends[:, 0:1], None, ALU.is_ge))
                for e in range(1, EXPERTS - 1):
                    link(nc.vector.scalar_tensor_tensor(out=tile_expert_f[:], in0=tile_ids_sb[:], scalar=ends[:, e:e + 1],
                                                        in1=tile_expert_f[:], op0=ALU.is_ge, op1=ALU.add))
                nc.vector.tensor_copy(tile_expert[:], tile_expert_f[:]).then_inc(experts_ready, 1)
                dve.wait_ge(experts_ready, 1)
                dve.wait_ge(tokens_in, 16)
                link(nc.vector.tensor_scalar(out_tokens[:], tokens[:], -float(T), None, ALU.add))

            @block.gpsimd
            def _(pool):
                pool.wait_ge(placed, 1)
                pool.wait_ge(table_cleared, 32)
                for t in range(NT):
                    pool.indirect_dma_start(table, bass.IndirectOffsetOnAxis(ap=place[:, t:t + 1], axis=0),
                                            token_ids_sb[:, t:t + 1], None).then_inc(scattered, 16)

        in_loop = ([now_ready, x_turned, x_drained, h_made, h_drained, h_turned, ht_drained, y_made, y_based, y_added])

        def over_rounds(r, i, n):
            return r * (16 * len(range(i, UNROLL, GATHERED))) + 16 * n

        with nc.Fori(0, TILES // UNROLL, 1) as r:
            with nc.Block() as block:
                @block.gpsimd
                def _(pool):
                    def gather(k):
                        if k >= GATHERED:
                            pool.wait_ge(y_added, k - GATHERED + 1)
                        pool.indirect_dma_start(
                            xg[:, k % GATHERED, :], None, rows,
                            bass.IndirectOffsetOnAxis(ap=now[:, k:k + 1], axis=0)).then_inc(gathered[k % GATHERED], 16)

                    def store(k):
                        pool.wait_ge(y_added, k + 1)
                        pool.indirect_dma_start(
                            out_rows, bass.IndirectOffsetOnAxis(ap=now_out[:, k:k + 1], axis=0),
                            yo[:, k % GATHERED, :], None, bounds_check=B * T - 1,
                            oob_is_err=False).then_inc(stored[k % GATHERED], 16)

                    nc.gpsimd.tensor_copy(now[:], tokens[:, bass.ds(r * UNROLL, UNROLL)]).then_inc(now_ready, 1)
                    nc.gpsimd.tensor_copy(now_out[:], out_tokens[:, bass.ds(r * UNROLL, UNROLL)]).then_inc(now_ready, 1)
                    pool.wait_ge(now_ready, 2)
                    for k in range(GATHERED):
                        gather(k)
                    for k in range(UNROLL):
                        store(k)
                        if k + GATHERED < UNROLL:
                            gather(k + GATHERED)
                    for i in range(GATHERED):
                        pool.wait_ge(stored[i], over_rounds(r, i, len(range(i, UNROLL, GATHERED))))

                @block.tensor
                def _(pe):
                    def turn_x(k):
                        pe.wait_ge(gathered[k % GATHERED], over_rounds(r, k % GATHERED, k // GATHERED + 1))
                        if k >= 2:
                            pe.wait_ge(x_drained, k - 1)
                        for c in range(DC):
                            last = nc.tensor.transpose(x_ps[k % 2][:, c * P:(c + 1) * P],
                                                       xg[:, k % GATHERED, c * P:(c + 1) * P], idf[:])
                        last.then_inc(x_turned, 1)

                    def hidden(k, e):
                        pe.wait_ge(x_drained, k + 1)
                        if k >= 1:
                            pe.wait_ge(h_drained, k)
                        for half in range(2):
                            for c in range(DC):
                                w = w1_sb[:, bass.ds(e, 1), c * HID + half * HALF:c * HID + (half + 1) * HALF]
                                last = nc.tensor.matmul(h_ps[:, half * HALF:(half + 1) * HALF],
                                                        xgt[:, k % 2, c * P:(c + 1) * P],
                                                        w.rearrange("p e n -> p (e n)"), start=c == 0, stop=c == DC - 1)
                        last.then_inc(h_made, 1)

                    def turn_h(k):
                        pe.wait_ge(h_drained, k + 1)
                        if k >= 1:
                            pe.wait_ge(ht_drained, k)
                        for c in range(HC):
                            last = nc.tensor.transpose(ht_ps[:, c, :], hs[:, k % 2, c * P:(c + 1) * P], idf[:])
                        last.then_inc(h_turned, 1)

                    def outputs(k, e):
                        pe.wait_ge(ht_drained, k + 1)
                        if k >= 2:
                            pe.wait_ge(y_added, k - 1)
                        for c in range(HC):
                            w = w2_sb[:, bass.ds(e, 1), c * D:(c + 1) * D]
                            last = nc.tensor.matmul(y_ps[k % 2][:, 0:D], hst[:, k % 2, c, :],
                                                    w.rearrange("p e n -> p (e n)"), start=c == 0, stop=c == HC - 1)
                        last.then_inc(y_made, 1)

                    experts = {}
                    turn_x(0)
                    pe.wait_ge(w_landed, 16 * (2 * EXPERTS + 2))
                    for k in range(UNROLL + 1):
                        if k < UNROLL:
                            experts[k] = pe.value_load(tile_expert[0:1, bass.ds(r * UNROLL + k, 1)], min_val=0,
                                                       max_val=EXPERTS - 1)
                            if k + 1 < UNROLL:
                                turn_x(k + 1)
                            hidden(k, experts[k])
                        if k >= 1:
                            outputs(k - 1, experts[k - 1])
                        if k < UNROLL:
                            turn_h(k)

                @block.scalar
                def _(act):
                    def move_x(k):
                        act.wait_ge(x_turned, k + 1)
                        if k >= 2:
                            act.wait_ge(h_made, k - 1)
                        for c in range(DC):
                            ins = nc.scalar.activation(xgt[:, k % 2, c * P:(c + 1) * P], x_ps[k % 2][:, c * P:(c + 1) * P],
                                                       ACT.Copy, scale=norms_sb[:, 1, c:c + 1])
                        ins.then_inc(x_drained, 1)

                    move_x(0)
                    for k in range(UNROLL):
                        if k + 1 < UNROLL:
                            move_x(k + 1)
                        act.wait_ge(h_turned, k + 1)
                        if k >= 2:
                            act.wait_ge(y_made, k - 1)
                        nc.scalar.activation(hst[:, k % 2], ht_ps[:], ACT.Relu).then_inc(ht_drained, 1)

                @block.vector
                def _(dve):
                    dve.wait_ge(w_landed, 16 * (2 * EXPERTS + 2))
                    for k in range(UNROLL + 1):
                        if k < UNROLL:
                            e = dve.value_load(tile_expert[0:1, bass.ds(r * UNROLL + k, 1)], min_val=0,
                                               max_val=EXPERTS - 1)
                            dve.wait_ge(h_made, k + 1)
                            if k >= 2:
                                dve.wait_ge(h_turned, k - 1)
                            nc.vector.tensor_tensor(hs[:, k % 2, :], h_ps[:],
                                                    b1_sb[:, bass.ds(e, 1), :].rearrange("p e n -> p (e n)"),
                                                    ALU.add).then_inc(h_drained, 1)
                            if k >= GATHERED:
                                dve.wait_ge(stored[k % GATHERED], over_rounds(r, k % GATHERED, k // GATHERED))
                            nc.vector.tensor_tensor(yo[:, k % GATHERED, :], xg[:, k % GATHERED, D:2 * D],
                                                    b2_sb[:, bass.ds(e, 1), :].rearrange("p e n -> p (e n)"),
                                                    ALU.add).then_inc(y_based, 1)
                        if k >= 1:
                            j = k - 1
                            dve.wait_ge(y_made, j + 1)
                            dve.wait_ge(y_based, j + 1)
                            nc.vector.tensor_tensor(yo[:, j % GATHERED, :], y_ps[j % 2][:, 0:D],
                                                    yo[:, j % GATHERED, :], ALU.add).then_inc(y_added, 1)

            for s in in_loop:
                nc.sync.sem_clear(s)
            nc.all_engine_barrier()


def kernel(L0_attn_x, L0_attn_w_qkv, L0_attn_w_out, L0_attn_b_out, L0_ffn_norm1_w, L0_ffn_norm2_w, L0_ffn_Wq,
           L0_ffn_Wdkv, L0_ffn_Wuk, L0_ffn_Wuv, L0_ffn_Wo, L0_ffn_ln_g, L0_ffn_ln_b, L0_ffn_gate_w, L0_ffn_gate_b,
           L0_ffn_W1, L0_ffn_b1, L0_ffn_W2, L0_ffn_b2):
    import ml_dtypes
    import numpy as np
    import concourse.bacc as bacc
    from concourse.bass_utils import run_bass_kernel_spmd

    def chunked(w):
        w = np.asarray(w)
        return np.ascontiguousarray(w.T.reshape(-1, P, w.shape[0]).transpose(1, 0, 2))

    def columns(v):
        v = np.asarray(v)
        v = v.reshape(*v.shape[:-1], -1, P)
        return np.ascontiguousarray(np.moveaxis(v, -1, 0))

    def every_partition(v):
        return np.ascontiguousarray(np.broadcast_to(np.asarray(v), (P, np.asarray(v).shape[-1])))

    f32 = np.float32
    half = HD // 2
    pos = np.arange(T, dtype=f32)
    i = np.arange(half, dtype=f32)
    theta0 = (10000.0 ** ((-2.0 * (i - 1.0) / HD).astype(np.float64))).astype(f32)
    theta1 = (1.0 / (10000.0 ** (np.arange(half) / half)).astype(f32)).astype(f32)
    row = np.arange(P)
    d = row % HD
    angle0 = (pos[None, :] * theta0[d // 2][:, None]).astype(np.float64)
    angle1 = (pos[None, :] * theta1[d % half][:, None]).astype(np.float64)
    sign0 = np.where(d % 2 == 0, 1.0, -1.0)[:, None]
    sign1 = np.where(d < half, -1.0, 1.0)[:, None]
    cos = np.stack([np.cos(angle0), np.cos(angle1)], 0).astype(f32)
    sin = np.stack([np.sin(angle0) * sign0, np.sin(angle1) * sign1], 0).astype(f32)
    perm = np.zeros((P, 2, P), f32)
    perm[row ^ 1, 0, row] = 1
    perm[row ^ half, 1, row] = 1
    ident = np.eye(P, dtype=f32)
    at = np.arange(P)
    keys_first = np.where(at[:, None] > at[None, :], MASKED, 0.0)
    mask = np.stack([keys_first, keys_first.T], 1)

    before = np.stack([at[:, None] < at[None, :], np.ones((P, P), bool)], 1).astype(f32)
    NT = B * TT
    token_ids = (T + at[:, None] + P * np.arange(NT)[None, :]).astype(np.uint32)

    W1, W2 = np.asarray(L0_ffn_W1), np.asarray(L0_ffn_W2)
    arrays = {
        "x": np.concatenate([np.asarray(L0_attn_x), np.asarray(L0_attn_x)[:1]]),
        "wqkv": chunked(L0_attn_w_qkv), "wout": chunked(L0_attn_w_out), "bout": every_partition(L0_attn_b_out),
        "norms": columns(np.stack([np.asarray(L0_ffn_norm1_w), np.asarray(L0_ffn_norm2_w)])),
        "wq": chunked(L0_ffn_Wq), "wdkv": chunked(L0_ffn_Wdkv), "wuk": chunked(L0_ffn_Wuk)[:, 0],
        "wuv": chunked(L0_ffn_Wuv)[:, 0], "wo": chunked(L0_ffn_Wo),
        "lnp": np.ascontiguousarray(np.stack([np.asarray(L0_ffn_ln_g), np.asarray(L0_ffn_ln_b)], 1)),
        "gate": chunked(L0_ffn_gate_w), "gate_b": every_partition(L0_ffn_gate_b),
        "w1": np.stack([chunked(W1[e]).reshape(P, -1) for e in range(EXPERTS)]),
        "b1": np.broadcast_to(np.asarray(L0_ffn_b1), (P, EXPERTS, HID)),
        "w2": np.stack([chunked(W2[e]).reshape(P, -1) for e in range(EXPERTS)]),
        "b2": np.broadcast_to(np.asarray(L0_ffn_b2), (P, EXPERTS, D)),
        "before": before, "starts": every_partition(np.arange(NT, dtype=f32) * P),
        "tile_ids": every_partition(np.arange(TILES, dtype=f32)), "token_ids": token_ids,
        "no_token": np.full((P, TILES), (B + 1) * T, np.uint32), "zero_row": np.zeros((1, 2 * D), f32),
        "cos": cos, "sin": sin, "perm": perm,
        "ident_f": ident, "ident_b": ident.astype(ml_dtypes.bfloat16), "mask_b": mask.astype(ml_dtypes.bfloat16),
    }
    nc = bacc.Bacc("TRN2", target_bir_lowering=False, num_devices=1)
    args = {}
    for name, a in arrays.items():
        arrays[name] = a = np.ascontiguousarray(a)
        args[name] = nc.dram_tensor("in_" + name, a.shape, mybir.dt.from_np(a.dtype), kind="ExternalInput").ap()
    out = nc.dram_tensor("out_x", (B, T, D), F32, kind="ExternalOutput").ap()
    build(nc, **args, out=out)
    r = run_bass_kernel_spmd(nc, [{"in_" + n: a for n, a in arrays.items()}], core_ids=[0])
    return r.results[0]["out_x"]
```
